# Optimizing a Trainium2 kernel written in Bass

```python
import numpy as np
import jax
import jax.numpy as jnp

def _softmax(x, axis=-1):
    return jax.nn.softmax(x, axis=axis)

def _gelu(x):
    return jax.nn.gelu(x, approximate=True)

def _silu(x):
    return jax.nn.silu(x)

def _sigmoid(x):
    return jax.nn.sigmoid(x)

def _layernorm(x, axis=-1, eps=1e-05):
    m = jnp.mean(x, axis=axis, keepdims=True)
    v = jnp.var(x, axis=axis, keepdims=True)
    return (x - m) / jnp.sqrt(v + eps)

def _scatter_add(tgt, idx, src, axis=0):
    return tgt.at[idx].add(src)

def _segment_sum(src, seg, n):
    return jax.ops.segment_sum(src, seg, n)
kernel_name = 'mk_sandwich_d1_jaxref_r8_a4a287'

def setup_inputs(seed: int=0):
    np.random.seed(seed)
    _w = jnp.asarray

    def _L0_attn_setup():
        import jax, jax.numpy as jnp
        import numpy as np
        from jax import lax
        D_MODEL, D_STATE, D_CONV, D_INNER, DT_RANK = (128, 16, 4, 256, 64)
        CHUNK = 32

        def _selective_scan(x, dt, A, Bp, Cp):
            Bb, L, d_inner = x.shape
            n_chunks = L // CHUNK

            def to_chunks(t):
                return t.reshape(Bb, n_chunks, CHUNK, t.shape[-1]).transpose(1, 2, 0, 3)
            xs, dts, Bs, Cs = (to_chunks(x), to_chunks(dt), to_chunks(Bp), to_chunks(Cp))

            def step(h, inp):
                x_i, dt_i, B_i, C_i = inp
                dA = jnp.exp(dt_i[..., None] * A)
                h = dA * h + dt_i[..., None] * B_i[:, None, :] * x_i[..., None]
                y = jnp.einsum('bds,bs->bd', h, C_i)
                return (h, y)

            def chunk_step(h, inp):
                h, ys = lax.scan(step, h, inp)
                return (lax.stop_gradient(h), ys)
            h0 = jnp.zeros((Bb, d_inner, D_STATE), dtype=x.dtype)
            _, ys = lax.scan(chunk_step, h0, (xs, dts, Bs, Cs))
            return ys.reshape(L, Bb, d_inner).transpose(1, 0, 2)
        key = jax.random.key(seed)
        ks = jax.random.split(key, 8)
        x = jax.random.normal(ks[0], (2, 512, D_MODEL), dtype=jnp.float32)
        W_in = jax.random.normal(ks[1], (D_MODEL, 2 * D_INNER), dtype=jnp.float32) * D_MODEL ** (-0.5)
        conv_w = jax.random.normal(ks[2], (D_INNER, 1, D_CONV), dtype=jnp.float32) * D_CONV ** (-0.5)
        conv_b = jax.random.normal(ks[3], (D_INNER,), dtype=jnp.float32) * 0.02
        W_x = jax.random.normal(ks[4], (D_INNER, DT_RANK + 2 * D_STATE), dtype=jnp.float32) * D_INNER ** (-0.5)
        W_dt = jax.random.uniform(ks[5], (DT_RANK, D_INNER), dtype=jnp.float32, minval=-DT_RANK ** (-0.5), maxval=DT_RANK ** (-0.5))
        dt = jnp.exp(jax.random.uniform(ks[6], (D_INNER,), dtype=jnp.float32) * (np.log(0.1) - np.log(0.001)) + np.log(0.001))
        b_dt = dt + jnp.log(-jnp.expm1(-dt))
        A_log = jnp.log(jnp.broadcast_to(jnp.arange(1, D_STATE + 1, dtype=jnp.float32), (D_INNER, D_STATE)))
        D = jnp.ones((D_INNER,), dtype=jnp.float32)
        W_out = jax.random.normal(ks[7], (D_INNER, D_MODEL), dtype=jnp.float32) * D_INNER ** (-0.5)
        return {'x': x, 'W_in': W_in, 'conv_w': conv_w, 'conv_b': conv_b, 'W_x': W_x, 'W_dt': W_dt, 'b_dt': b_dt, 'A_log': A_log, 'D': D, 'W_out': W_out}
    _L0_attn_in = _L0_attn_setup()

    def _L0_ffn_setup():
        import jax, jax.numpy as jnp
        import numpy as np
        HIDDEN = 128
        N_EXPERTS = 8
        TOP_K = 2
        INTER = 176
        N_SHARED = 2
        SCALE = 1.0
        key = jax.random.key(seed)
        ks = jax.random.split(key, 9)
        s_h = 1.0 / np.sqrt(HIDDEN)
        s_i = 1.0 / np.sqrt(INTER)
        x = jax.random.normal(ks[0], (2, 256, HIDDEN), dtype=jnp.float32)
        gate_w = jax.random.uniform(ks[1], (N_EXPERTS, HIDDEN), jnp.float32, -s_h, s_h)
        wg = jax.random.uniform(ks[2], (N_EXPERTS, HIDDEN, INTER), jnp.float32, -s_h, s_h)
        wu = jax.random.uniform(ks[3], (N_EXPERTS, HIDDEN, INTER), jnp.float32, -s_h, s_h)
        wd = jax.random.uniform(ks[4], (N_EXPERTS, INTER, HIDDEN), jnp.float32, -s_i, s_i)
        si = INTER * N_SHARED
        s_si = 1.0 / np.sqrt(si)
        swg = jax.random.uniform(ks[5], (HIDDEN, si), jnp.float32, -s_h, s_h)
        swu = jax.random.uniform(ks[6], (HIDDEN, si), jnp.float32, -s_h, s_h)
        swd = jax.random.uniform(ks[7], (si, HIDDEN), jnp.float32, -s_si, s_si)
        return {'x': x, 'gate_w': gate_w, 'wg': wg, 'wu': wu, 'wd': wd, 'swg': swg, 'swu': swu, 'swd': swd}
    _L0_ffn_in = _L0_ffn_setup()
    _d = {'L0_attn_x': _L0_attn_in['x'], 'L0_attn_W_in': _L0_attn_in['W_in'], 'L0_attn_conv_w': _L0_attn_in['conv_w'], 'L0_attn_conv_b': _L0_attn_in['conv_b'], 'L0_attn_W_x': _L0_attn_in['W_x'], 'L0_attn_W_dt': _L0_attn_in['W_dt'], 'L0_attn_b_dt': _L0_attn_in['b_dt'], 'L0_attn_A_log': _L0_attn_in['A_log'], 'L0_attn_D': _L0_attn_in['D'], 'L0_attn_W_out': _L0_attn_in['W_out'], 'L0_ffn_gate_w': _L0_ffn_in['gate_w'], 'L0_ffn_wg': _L0_ffn_in['wg'], 'L0_ffn_wu': _L0_ffn_in['wu'], 'L0_ffn_wd': _L0_ffn_in['wd'], 'L0_ffn_swg': _L0_ffn_in['swg'], 'L0_ffn_swu': _L0_ffn_in['swu'], 'L0_ffn_swd': _L0_ffn_in['swd']}
    _x0 = _d['L0_attn_x']
    _d['L0_attn_x'] = jax.random.normal(jax.random.fold_in(jax.random.key(seed), 1), (8, 512, 128), dtype=_x0.dtype)
    del _x0
    return _d

def reference(L0_attn_x, L0_attn_W_in, L0_attn_conv_w, L0_attn_conv_b, L0_attn_W_x, L0_attn_W_dt, L0_attn_b_dt, L0_attn_A_log, L0_attn_D, L0_attn_W_out, L0_ffn_gate_w, L0_ffn_wg, L0_ffn_wu, L0_ffn_wd, L0_ffn_swg, L0_ffn_swu, L0_ffn_swd):

    def _L0_attn_ref(x, W_in, conv_w, conv_b, W_x, W_dt, b_dt, A_log, D, W_out):
        import jax, jax.numpy as jnp
        import numpy as np
        from jax import lax
        D_MODEL, D_STATE, D_CONV, D_INNER, DT_RANK = (128, 16, 4, 256, 64)
        CHUNK = 32

        def _selective_scan(x, dt, A, Bp, Cp):
            Bb, L, d_inner = x.shape
            n_chunks = L // CHUNK

            def to_chunks(t):
                return t.reshape(Bb, n_chunks, CHUNK, t.shape[-1]).transpose(1, 2, 0, 3)
            xs, dts, Bs, Cs = (to_chunks(x), to_chunks(dt), to_chunks(Bp), to_chunks(Cp))

            def step(h, inp):
                x_i, dt_i, B_i, C_i = inp
                dA = jnp.exp(dt_i[..., None] * A)
                h = dA * h + dt_i[..., None] * B_i[:, None, :] * x_i[..., None]
                y = jnp.einsum('bds,bs->bd', h, C_i)
                return (h, y)

            def chunk_step(h, inp):
                h, ys = lax.scan(step, h, inp)
                return (lax.stop_gradient(h), ys)
            h0 = jnp.zeros((Bb, d_inner, D_STATE), dtype=x.dtype)
            _, ys = lax.scan(chunk_step, h0, (xs, dts, Bs, Cs))
            return ys.reshape(L, Bb, d_inner).transpose(1, 0, 2)
        Bb, L, _ = x.shape
        xz = x @ W_in
        xi, z = jnp.split(xz, 2, axis=-1)
        xc = xi.transpose(0, 2, 1)
        xc = lax.conv_general_dilated(xc, conv_w, window_strides=(1,), padding=[(D_CONV - 1, 0)], dimension_numbers=('NCH', 'OIH', 'NCH'), feature_group_count=D_INNER)
        xc = (xc + conv_b[None, :, None]).transpose(0, 2, 1)
        xc = jax.nn.silu(xc)
        xp = xc @ W_x
        dt_r, Bp, Cp = jnp.split(xp, [DT_RANK, DT_RANK + D_STATE], axis=-1)
        dt = jax.nn.softplus(dt_r @ W_dt + b_dt)
        A = -jnp.exp(A_log)
        y = _selective_scan(xc, dt, A, Bp, Cp)
        y = y + xc * D
        y = y * jax.nn.silu(z)
        return y @ W_out

    def _L0_ffn_ref(x, gate_w, wg, wu, wd, swg, swu, swd):
        import jax, jax.numpy as jnp
        import numpy as np
        HIDDEN = 128
        N_EXPERTS = 8
        TOP_K = 2
        INTER = 176
        N_SHARED = 2
        SCALE = 1.0
        B, S, H = x.shape
        xf = x.reshape(-1, H)
        T = xf.shape[0]
        logits = xf.astype(jnp.float32) @ gate_w.astype(jnp.float32).T
        scores = jax.nn.softmax(logits, axis=-1)
        topw, topi = jax.lax.top_k(scores, TOP_K)
        denom = topw.sum(axis=-1, keepdims=True) + 1e-20
        topw = topw / denom * SCALE
        wdense = jnp.zeros((T, N_EXPERTS), jnp.float32).at[jnp.arange(T)[:, None], topi].set(topw)
        hg = jnp.einsum('th,ehi->eti', xf, wg)
        hu = jnp.einsum('th,ehi->eti', xf, wu)
        eo = jnp.einsum('eti,eih->eth', jax.nn.silu(hg) * hu, wd)
        y = jnp.einsum('te,eth->th', wdense, eo)
        shared = jax.nn.silu(xf @ swg) * (xf @ swu) @ swd
        return (y + shared).reshape(B, S, H)
    x = L0_attn_x
    x = x + _layernorm(_L0_attn_ref(_layernorm(x, axis=-1), L0_attn_W_in, L0_attn_conv_w, L0_attn_conv_b, L0_attn_W_x, L0_attn_W_dt, L0_attn_b_dt, L0_attn_A_log, L0_attn_D, L0_attn_W_out), axis=-1)
    x = x + _layernorm(_L0_ffn_ref(_layernorm(x, axis=-1), L0_ffn_gate_w, L0_ffn_wg, L0_ffn_wu, L0_ffn_wd, L0_ffn_swg, L0_ffn_swu, L0_ffn_swd), axis=-1)
    return x

_drawn_inputs = setup_inputs


def setup_inputs(seed=0):
    import zlib

    import numpy as np

    out = dict(_drawn_inputs(seed))
    spreads = {'L0_attn_D': (1.0, 0.2)}
    factors = {}
    for name, (base, spread) in spreads.items():
        noise = np.random.default_rng([zlib.crc32(name.encode()), seed]).standard_normal(out[name].shape)
        drawn = base * np.exp(spread * noise) if base else spread * noise
        out[name] = jnp.asarray(drawn.astype(out[name].dtype))
    for name, factor in factors.items():
        out[name] = (out[name] * factor).astype(out[name].dtype)
    return out
```

```python
import concourse.bass as bass
from concourse import mybir
from contextlib import ExitStack

F32 = mybir.dt.float32
ALU = mybir.AluOpType
ACT = mybir.ActivationFunctionType
AX = mybir.AxisListType


def begun(value):
    return not isinstance(value, int) or value > 0


def layer_kernel(nc, x, W_in, conv_w, conv_b, W_x, W_dt, b_dt, A_log, D, W_out,
                 gate_w, wg, wu, wd, swg, swu, swd, out):
    P = 128
    NB, L, DM = x.shape
    DI = conv_w.shape[0]
    NH = DI // P
    TAPS = conv_w.shape[2]
    NS = A_log.shape[1]
    DR = W_dt.shape[0]
    XP = DR + 2 * NS
    NE, _, FE = wg.shape
    FS = swg.shape[1]
    NQ = L // P
    GS = 4
    NG = NS // GS
    UNITS = NG * NH
    RING = 4
    BC = 2
    QE = P // NE
    SHARED = [min(P, FS - P * j) for j in range((FS + P - 1) // P)]
    NSH = len(SHARED)
    TILES = NSH + FE // QE
    HALF = TILES // 2
    ROUTED = TILES - NSH
    AR = 5
    LAG = 3
    EPS = 1e-5
    assert DM == P and UNITS % RING == 0 and NG % BC == 0 and TILES % 2 == 0
    assert FE == ROUTED * QE and NH == 2 and NQ == 4

    with ExitStack() as ctx:
        def sb(name, shape, dtype=F32):
            return ctx.enter_context(nc.sbuf_tensor(name, shape, dtype))

        def psum(name, shape):
            return ctx.enter_context(nc.psum_tensor(name, shape, F32))

        def sem(name):
            return ctx.enter_context(nc.semaphore(name))

        w_in = sb("w_in", [P, 2 * DI])
        w_x = sb("w_x", [P, NH, XP])
        w_dt = sb("w_dt", [DR, DI])
        w_out = sb("w_out", [P, NH, DM])
        cw = sb("cw", [P, NH, TAPS])
        cb = sb("cb", [P, NH])
        bdt = sb("bdt", [P, NH])
        a_neg = sb("a_neg", [P, NH, NS])
        a_exp = sb("a_exp", [P, NH, NS])
        d_skip = sb("d_skip", [P, NH])
        gate = sb("gate", [P, NE])
        w_gate = sb("w_gate", [P, P, ROUTED])
        w_up = sb("w_up", [P, P, ROUTED])
        w_down = sb("w_down", [P, ROUTED, DM])
        s_gate = sb("s_gate", [P, FS])
        s_up = sb("s_up", [P, FS])
        s_down = sb("s_down", [P, NSH, DM])
        ident = sb("ident", [P, P])
        lower = sb("lower", [P, NQ, NE, NE])
        neg_half = sb("neg_half", [P, NQ])
        waited = sb("waited", [P, 1])
        xln = sb("xln", [P, NQ, DM])
        xn = sb("xn", [P, NQ, DM])
        xnT = sb("xnT", [P, L])
        stA = sb("stA", [P, NQ, 6])
        mvA = sb("mvA", [P, NQ, 2])
        rsA = sb("rsA", [P, NQ])
        xi_pad = sb("xi_pad", [P, NH, L + TAPS - 1])
        conv0 = sb("conv0", [P, NH, L])
        conv1 = sb("conv1", [P, NH, L])
        xc = sb("xc", [P, NH, L])
        xcD = sb("xcD", [P, NH, L])
        xproj = sb("xproj", [XP, L])
        dt = sb("dt", [P, NH, L])
        u = sb("u", [P, NH, L])
        dA = sb("dA", [P, RING, GS, L])
        hb = sb("hb", [P, RING, GS, L])
        b_all = sb("b_all", [P, BC, GS, L])
        c_all = sb("c_all", [P, BC, GS, L])
        zg = sb("zg", [P, NQ, DI])
        yg = sb("yg", [P, NQ, DI])
        ygT = sb("ygT", [P, NH, L])
        sp_r = yg[:].rearrange("p q d -> p (q d)").rearrange("p (h l) -> p h l", h=NH)
        sp_t = ygT
        xres = sb("xres", [P, NQ, DM])
        o_sb = sb("o_sb", [P, NQ, DM])
        stO = sb("stO", [P, NQ, 6])
        mvO = sb("mvO", [P, NQ, 2])
        rsO = sb("rsO", [P, NQ])
        st2 = sb("st2", [P, NQ, 6])
        mv2 = sb("mv2", [P, NQ, 2])
        rs2 = sb("rs2", [P, NQ])
        x1 = sb("x1", [P, NQ, DM])
        x1n = sb("x1n", [P, NQ, DM])
        x1T = sb("x1T", [P, L])
        r_max = sb("r_max", [P, NQ])
        r_sh = sb("r_sh", [P, NQ, NE])
        r_ex = sb("r_ex", [P, NQ, NE])
        r_sum = sb("r_sum", [P, NQ])
        r_inv = sb("r_inv", [P, NQ])
        r_sc = sb("r_sc", [P, NQ, NE])
        r_gt = sb("r_gt", [P, NQ, NE, NE])
        r_eq = sb("r_eq", [P, NQ, NE, NE])
        r_rank = sb("r_rank", [P, NQ, NE])
        r_top = sb("r_top", [P, NQ, NE])
        r_den = sb("r_den", [P, NQ])
        r_rden = sb("r_rden", [P, NQ])
        w_tok = sb("w_tok", [P, NQ, P])
        w_feat = sb("w_feat", [P, L])
        silu_g = sb("silu_g", [P, 2, L])
        act = sb("act", [P, AR, L])
        x1_old = sb("x1_old", [P, NQ, DM])
        stG = sb("stG", [P, NQ, 6])
        mvG = sb("mvG", [P, NQ, 2])
        rsG = sb("rsG", [P, NQ])
        y_out = sb("y_out", [P, NQ, DM])

        bc_dram = nc.dram_tensor("bc_dram", (NB, 2 * NS, L), F32, kind="Internal").ap()

        y_ps = psum("y_ps", [P, NQ, DI])
        misc_bank = psum("misc_bank", [P, L])
        g_ps = psum("g_ps", [P, 2, L])
        u_ps = psum("u_ps", [P, 2, L])
        f_ps = psum("f_ps", [P, NQ, DM])

        early_loaded, late_loaded = sem("early_loaded"), sem("late_loaded")
        xln_loaded, xres_loaded = sem("xln_loaded"), sem("xres_loaded")
        bc_stored, x1_moved, y_stored = sem("bc_stored"), sem("x1_moved"), sem("y_stored")
        b_loaded = [sem(f"b_loaded{g}") for g in range(BC)]
        c_loaded = [sem(f"c_loaded{g}") for g in range(BC)]
        const_step, const_ready, a_ready_exp, a_ready = sem("const_step"), sem("const_ready"), sem("a_ready_exp"), sem("a_ready")
        zeros_ready, waited_step = sem("zeros_ready"), sem("waited_step")
        lnA_step, varA_ready, rsA_ready, xn_ready = sem("lnA_step"), sem("varA_ready"), sem("rsA_ready"), sem("xn_ready")
        xnT_ps, xnT_ready = sem("xnT_ps"), sem("xnT_ready")
        xi_ps, xi_ready, conv_step = sem("xi_ps"), sem("xi_ready"), sem("conv_step")
        xc_ready, xcD_ready = sem("xc_ready"), sem("xcD_ready")
        xp_ps, xp_ready = sem("xp_ps"), sem("xp_ready")
        dt_ps, dt_taken, sp_step, sp_ready = sem("dt_ps"), sem("dt_taken"), sem("sp_step"), sem("sp_ready")
        dt_step, dt_ready, u_ready = sem("dt_step"), sem("dt_ready"), sem("u_ready")
        z_ps, z_ready = sem("z_ps"), sem("z_ready")
        dA_ready, bu_ready, scan_done, hc_ready, sum_done = (
            sem("dA_ready"), sem("bu_ready"), sem("scan_done"), sem("hc_ready"), sem("sum_done"))
        yg_ready, yT_ps, yT_ready, o_ps, o_ready = (
            sem("yg_ready"), sem("yT_ps"), sem("yT_ready"), sem("o_ps"), sem("o_ready"))
        lnO_step, varO_ready, rsO_ready, on_ready = sem("lnO_step"), sem("varO_ready"), sem("rsO_ready"), sem("on_ready")
        x1_ready = sem("x1_ready")
        ln2_step, var2_ready, rs2_ready, x1n_ready = sem("ln2_step"), sem("var2_ready"), sem("rs2_ready"), sem("x1n_ready")
        x1T_ps, x1T_ready, lg_ps, lg_taken = sem("x1T_ps"), sem("x1T_ready"), sem("lg_ps"), sem("lg_taken")
        rt_step, rex_ready, w_ready, wf_ps, wf_ready = (
            sem("rt_step"), sem("rex_ready"), sem("w_ready"), sem("wf_ps"), sem("wf_ready"))
        gate_ps, up_ps, silu_ready, act_ready, actw_ready, down_done = (
            sem("gate_ps"), sem("up_ps"), sem("silu_ready"), sem("act_ready"), sem("actw_ready"), sem("down_done"))
        lnG_step, varG_ready, rsG_ready, f_taken, y_ready = (
            sem("lnG_step"), sem("varG_ready"), sem("rsG_ready"), sem("f_taken"), sem("y_ready"))

        tokens = lambda ap: ap.rearrange("(q p) m -> p q m", p=P)
        halves = lambda ap: ap.rearrange("(h p) n -> p h n", p=P)

        LN_STEPS = 2 * NQ
        CONV_STEPS = NH * (TAPS - 1)
        DT_STEPS = 2
        RT_STEPS = 13
        EARLY, LATE = 10, 5 + NSH

        def plan(i):
            return (i + 1 < NB, 0 <= i < NB, 0 <= i - 1 < NB, 0 <= i - 2 < NB)

        def run(engine, iteration):
            for i in (-1, 0, 1):
                iteration(i, *plan(i))
            with engine.Fori(2, NB - 1) as i:
                iteration(i, True, True, True, True)
            for i in (NB - 1, NB, NB + 1):
                iteration(i, *plan(i))

        block = ctx.enter_context(nc.Block())

        @block.sync
        def _(sp):
            def load_x(b):
                if begun(NQ * b):
                    sp.wait_ge(xn_ready, NQ * b)
                sp.dma_start(xln[:], tokens(x[b])).then_inc(xln_loaded, 16)

            load_x(0)
            for to, of in ((w_in[:], W_in), (w_x[:], halves(W_x)), (w_dt[:], W_dt),
                           (cw[:], conv_w.rearrange("(h p) o k -> p h (o k)", p=P)),
                           (cb[:], conv_b.rearrange("(h p) -> p h", p=P)),
                           (bdt[:], b_dt.rearrange("(h p) -> p h", p=P)),
                           (d_skip[:], D.rearrange("(h p) -> p h", p=P)),
                           (a_exp[:], halves(A_log)),
                           (w_out[:], halves(W_out)),
                           (gate[:], gate_w.rearrange("e m -> m e"))):
                with nc.allow_non_contiguous_dma(reason="a few small vectors, once"):
                    sp.dma_start(to, of).then_inc(early_loaded, 16)

            def late_weights():
                sp.dma_start(w_gate[:].rearrange("p f j -> p (f j)").rearrange("p (e r) -> p e r", e=NE),
                             wg.rearrange("e m r -> m e r")).then_inc(late_loaded, 16)
                sp.dma_start(w_up[:].rearrange("p f j -> p (f j)").rearrange("p (e r) -> p e r", e=NE),
                             wu.rearrange("e m r -> m e r")).then_inc(late_loaded, 16)
                sp.dma_start(s_gate[:], swg).then_inc(late_loaded, 16)
                sp.dma_start(s_up[:], swu).then_inc(late_loaded, 16)
                for j, n in enumerate(SHARED):
                    sp.dma_start(s_down[0:n, j, :], swd[P * j:P * j + n, :]).then_inc(late_loaded, 16)
                sp.dma_start(w_down[:], wd.rearrange("e r h -> (e r) h").rearrange("(p j) h -> p j h", p=P))\
                  .then_inc(late_loaded, 16)

            def bc_group(b, g):
                rows = GS * L
                if begun(UNITS * b + NH * (g - BC + 1)):
                    sp.wait_ge(bu_ready, UNITS * b + NH * (g - BC + 1))
                sp.dma_start(b_all[:, g % BC].rearrange("p s l -> p (s l)"),
                             bc_dram[b, GS * g:GS * g + GS, :].rearrange("s l -> (s l)").unsqueeze(0)
                             .broadcast_to([P, rows])).then_inc(b_loaded[g % BC], 16)
                if begun(UNITS * b + NH * (g - BC + 1)):
                    sp.wait_ge(hc_ready, UNITS * b + NH * (g - BC + 1))
                sp.dma_start(c_all[:, g % BC].rearrange("p s l -> p (s l)"),
                             bc_dram[b, NS + GS * g:NS + GS * g + GS, :].rearrange("s l -> (s l)").unsqueeze(0)
                             .broadcast_to([P, rows])).then_inc(c_loaded[g % BC], 16)

            def iteration(i, doA, doS, doO, doG, doL):
                if doO:
                    if begun(i - 1):
                        sp.wait_ge(x1_ready, i - 1)
                    sp.dma_start(xres[:], tokens(x[i - 1])).then_inc(xres_loaded, 16)
                if doS:
                    bc_group(i, 2)
                if doA:
                    sp.wait_ge(xp_ready, i + 2)
                    sp.dma_start(bc_dram[i + 1], xproj[DR:XP, :]).then_inc(bc_stored, 16)
                if doS:
                    bc_group(i, 3)
                if doL:
                    load_x(i + 2)
                if doG:
                    sp.wait_ge(y_ready, i - 1)
                    sp.dma_start(tokens(out[i - 2]), y_out[:]).then_inc(y_stored, 16)
                if doO:
                    sp.wait_ge(x1_ready, i)
                    sp.dma_start(x1_old[:], x1[:]).then_inc(x1_moved, 16)
                if doA:
                    sp.wait_ge(bc_stored, 16 * (i + 2))
                    bc_group(i + 1, 0)
                    bc_group(i + 1, 1)

            late_weights()
            for i in (-1, 0, 1):
                iteration(i, *plan(i), True)
            with sp.Fori(2, NB - 2) as i:
                iteration(i, True, True, True, True, True)
            for i in (NB - 2, NB - 1, NB, NB + 1):
                iteration(i, *plan(i), False)
            sp.wait_ge(y_stored, 16 * NB)

        @block.gpsimd
        def _(pool):
            nc.gpsimd.memset(neg_half[:], -0.5).then_inc(const_step, 1)
            nc.gpsimd.memset(ident[:], 0.0).then_inc(const_step, 1)
            nc.gpsimd.memset(lower[:], 1.0).then_inc(const_step, 1)
            pool.wait_ge(const_step, 3)
            nc.gpsimd.affine_select(out=ident[:], in_=ident[:], compare_op=ALU.not_equal, fill=1.0, base=0,
                                    pattern=[[-1, P]], channel_multiplier=1).then_inc(const_ready, 1)
            nc.gpsimd.affine_select(out=lower[:], in_=lower[:], compare_op=ALU.is_gt, fill=0.0, base=0,
                                    pattern=[[0, NQ], [1, NE], [-1, NE]], channel_multiplier=0).then_inc(const_ready, 1)

            def power(rs, ready, done, n):
                pool.wait_ge(ready, n)
                nc.gpsimd.tensor_tensor(rs[:], rs[:], neg_half[:], ALU.pow).then_inc(done, 1)

            def bu(b, k):
                n = UNITS * b + k
                g, h = k // NH, k % NH
                if h == 0:
                    pool.wait_ge(b_loaded[g % BC], 16 * (NG // BC * b + g // BC + 1))
                if begun(n + 1 - RING):
                    pool.wait_ge(sum_done, n + 1 - RING)
                nc.gpsimd.tensor_tensor(hb[:, k % RING], u[:, h, :].unsqueeze(1).broadcast_to([P, GS, L]),
                                        b_all[:, g % BC], ALU.mult).then_inc(bu_ready, 1)

            def weigh(b, j):
                pool.wait_ge(act_ready, TILES * b + j + 1)
                if j == NSH:
                    pool.wait_ge(wf_ready, b + 1)
                nc.gpsimd.tensor_tensor(act[:, j % AR], act[:, j % AR], w_feat[:], ALU.mult).then_inc(actw_ready, 1)

            def make_u(b):
                pool.wait_ge(dt_ready, b + 1)
                pool.wait_ge(xc_ready, NH * (b + 1))
                if begun(UNITS * b):
                    pool.wait_ge(bu_ready, UNITS * b)
                nc.gpsimd.tensor_tensor(u[:], dt[:], xc[:], ALU.mult).then_inc(u_ready, 1)
                pool.wait_ge(u_ready, b + 1)

            def iteration(i, doA, doS, doO, doG):
                a, o, g = i + 1, i - 1, i - 2
                if doA:
                    power(rsA, varA_ready, rsA_ready, a + 1)
                if doS:
                    bu(i, 1)
                if doG:
                    weigh(g, 7)
                if doS:
                    bu(i, 2)
                if doG:
                    weigh(g, 8)
                    weigh(g, 9)
                if doO:
                    power(rsO, varO_ready, rsO_ready, o + 1)
                if doS:
                    bu(i, 3)
                if doG:
                    weigh(g, 10)
                    weigh(g, 11)
                if doO:
                    power(rs2, var2_ready, rs2_ready, o + 1)
                if doG:
                    weigh(g, 12)
                    weigh(g, 13)
                if doS:
                    bu(i, 4)
                if doG:
                    power(rsG, varG_ready, rsG_ready, g + 1)
                if doS:
                    bu(i, 5)
                    bu(i, 6)
                if doO:
                    weigh(o, 3)
                if doS:
                    bu(i, 7)
                if doA:
                    make_u(a)
                if doO:
                    weigh(o, 4)
                if doA:
                    bu(a, 0)
                if doO:
                    weigh(o, 5)
                    weigh(o, 6)

            run(pool, iteration)

        @block.scalar
        def _(acte):
            A = nc.scalar
            acte.wait_ge(early_loaded, 16 * EARLY)
            A.activation(a_neg[:], a_exp[:], ACT.Exp).then_inc(a_ready_exp, 1)

            def discount(b, k):
                n = UNITS * b + k
                g, h = k // NH, k % NH
                if begun(n + 1 - RING):
                    acte.wait_ge(scan_done, n + 1 - RING)
                if k == 0:
                    acte.wait_ge(dt_ready, b + 1)
                for s in range(GS):
                    done = A.activation(dA[:, k % RING, s, 1:L], dt[:, h, 1:L], ACT.Exp,
                                        scale=a_neg[:, h, GS * g + s:GS * g + s + 1])
                done.then_inc(dA_ready, 1)

            def silu_tile(b, j):
                n = TILES * b + j
                rows = SHARED[j] if j < NSH else P
                acte.wait_ge(gate_ps, n + 1)
                if begun(n - 1):
                    acte.wait_ge(act_ready, n - 1)
                A.activation(silu_g[0:rows, j % 2], g_ps[0:rows, j % 2], ACT.Silu).then_inc(silu_ready, 1)

            def iteration(i, doA, doS, doO, doG):
                a, o, g = i + 1, i - 1, i - 2
                if doO:
                    for h in range(NH):
                        acte.wait_ge(yT_ps, NH * o + h + 1)
                        if begun(o):
                            acte.wait_ge(o_ps, o)
                        A.copy(ygT[:, h], misc_bank[:]).then_inc(yT_ready, 1)
                if doS:
                    for m in range(2):
                        acte.wait_ge(z_ps, 2 * i + m + 1)
                        if begun(i):
                            acte.wait_ge(yg_ready, i)
                        A.activation(zg[:, 2 * m:2 * m + 2].rearrange("p q d -> p (q d)"), misc_bank[:],
                                     ACT.Silu).then_inc(z_ready, 1)
                if doO:
                    acte.wait_ge(o_ps, o + 1)
                    A.copy(o_sb[:].rearrange("p q m -> p (q m)"), misc_bank[:]).then_inc(o_ready, 1)
                if doG:
                    silu_tile(g, 7)
                    silu_tile(g, 8)
                if doA:
                    acte.wait_ge(xnT_ps, a + 1)
                    A.copy(xnT[:], misc_bank[:]).then_inc(xnT_ready, 1)
                if doG:
                    silu_tile(g, 9)
                for h in range(NH):
                    if doA:
                        acte.wait_ge(xi_ps, NH * a + h + 1)
                        if begun(a):
                            acte.wait_ge(dt_ready, a)
                        A.activation(conv0[:, h], misc_bank[:], ACT.Identity, bias=cb[:, h:h + 1],
                                     scale=cw[:, h, TAPS - 1:TAPS])
                        A.copy(xi_pad[:, h, TAPS - 1:], misc_bank[:]).then_inc(xi_ready, 1)
                    if h == 0 and doG:
                        silu_tile(g, 10)
                if doG:
                    silu_tile(g, 11)
                for h in range(NH):
                    if doA:
                        acte.wait_ge(conv_step, CONV_STEPS * a + (TAPS - 1) * (h + 1))
                        if begun(a):
                            acte.wait_ge(u_ready, a)
                        A.activation(xc[:, h], conv1[:, h], ACT.Silu).then_inc(xc_ready, 1)
                    if h == 0 and doG:
                        silu_tile(g, 12)
                if doA:
                    acte.wait_ge(xc_ready, NH * (a + 1))
                    if begun(UNITS * (a - 1) + 1):
                        acte.wait_ge(sum_done, UNITS * (a - 1) + 1)
                    for h in range(NH):
                        A.activation(xcD[:, h], xc[:, h], ACT.Copy, scale=d_skip[:, h:h + 1]).then_inc(xcD_ready, 1)
                if doG:
                    silu_tile(g, 13)
                if doA:
                    acte.wait_ge(xp_ps, a + 1)
                    if begun(NH * a):
                        acte.wait_ge(dt_ps, NH * a)
                    if begun(16 * a):
                        acte.wait_ge(bc_stored, 16 * a)
                    A.copy(xproj[:], misc_bank[0:XP, :]).then_inc(xp_ready, 1)
                if doO:
                    acte.wait_ge(x1T_ps, o + 1)
                    if begun(TILES * o):
                        acte.wait_ge(up_ps, TILES * o)
                    A.copy(x1T[:], misc_bank[:]).then_inc(x1T_ready, 1)
                if doS:
                    for k in range(4, 8):
                        discount(i, k)
                if doA:
                    for h in range(NH):
                        acte.wait_ge(dt_ps, NH * a + h + 1)
                        A.activation(sp_t[:, h], misc_bank[:], ACT.Abs, bias=bdt[:, h:h + 1])
                        A.activation(sp_r[:, h], misc_bank[:], ACT.Relu, bias=bdt[:, h:h + 1]).then_inc(dt_taken, 1)
                    acte.wait_ge(dt_taken, NH * (a + 1))
                    A.activation(sp_t[:], sp_t[:], ACT.Exp, scale=-1.0).then_inc(sp_step, 1)
                    acte.wait_ge(sp_step, 2 * a + 1)
                    A.activation(conv0[:], sp_t[:], ACT.Identity, bias=1.0).then_inc(sp_step, 1)
                    acte.wait_ge(sp_step, 2 * a + 2)
                    A.activation(conv1[:], conv0[:], ACT.Ln).then_inc(sp_ready, 1)
                if doO:
                    acte.wait_ge(lg_taken, o + 1)
                    A.activation(r_ex[:], r_sh[:], ACT.Exp).then_inc(rex_ready, 1)
                    for j in range(2):
                        silu_tile(o, j)
                    acte.wait_ge(wf_ps, o + 1)
                    if begun(ROUTED * o):
                        acte.wait_ge(actw_ready, ROUTED * o)
                    A.copy(w_feat[:], misc_bank[:]).then_inc(wf_ready, 1)
                    for j in range(2, HALF):
                        silu_tile(o, j)
                if doA:
                    for k in range(4):
                        discount(a, k)

            run(acte, iteration)

        @block.vector
        def _(dve):
            V = nc.vector
            V.memset(dA[:, :, :, 0:1], 0.0).then_inc(zeros_ready, 1)
            V.memset(xi_pad[:, :, 0:TAPS - 1], 0.0).then_inc(zeros_ready, 1)
            dve.wait_ge(a_ready_exp, 1)
            dve.wait_ge(zeros_ready, 2)
            V.tensor_scalar(a_neg[:], a_neg[:], -1.0, None, ALU.mult).then_inc(a_ready, 1)
            dve.wait_ge(a_ready, 1)
            dve.wait_ge(const_ready, 2)

            def stats(src, st, mv, rs, step, ready, b):
                for q in range(NQ):
                    V.bn_stats(st[:, q], src[:, q]).then_inc(step, 1)
                dve.wait_ge(step, LN_STEPS * b + NQ)
                V.memset(waited[:], 0.0).then_inc(waited_step, 1)
                for q in range(NQ):
                    V.bn_aggr(mv[:, q], st[:, q]).then_inc(step, 1)
                dve.wait_ge(step, LN_STEPS * b + 2 * NQ)
                V.tensor_scalar(rs[:], mv[:, :, 1], EPS, None, ALU.add).then_inc(ready, 1)

            def normalize(dst, src, mv, rs, done=None):
                for q in range(NQ):
                    last = V.tensor_scalar(dst[:, q], src[:, q], mv[:, q, 0:1], rs[:, q:q + 1],
                                           ALU.subtract, ALU.mult)
                    if done is not None:
                        last.then_inc(done, 1)
                return last

            def scan(b, k):
                n = UNITS * b + k
                dve.wait_ge(dA_ready, n + 1)
                dve.wait_ge(bu_ready, n + 1)
                h_of = hb[:, k % RING].rearrange("p s l -> p (s l)")
                V.tensor_tensor_scan(h_of, dA[:, k % RING].rearrange("p s l -> p (s l)"), h_of, 0.0,
                                     ALU.mult, ALU.add).then_inc(scan_done, 1)

            def times_c(b, k):
                n = UNITS * b + k
                g = k // NH
                if k % NH == 0:
                    dve.wait_ge(c_loaded[g % BC], 16 * (NG // BC * b + g // BC + 1))
                dve.wait_ge(scan_done, n + 1)
                V.tensor_tensor(hb[:, k % RING], hb[:, k % RING], c_all[:, g % BC], ALU.mult).then_inc(hc_ready, 1)

            def conv(b, h):
                dve.wait_ge(xi_ready, NH * b + h + 1)
                src, dst = conv0, conv1
                for m, tap in enumerate(range(TAPS - 2, -1, -1)):
                    if m:
                        dve.wait_ge(conv_step, CONV_STEPS * b + (TAPS - 1) * h + m)
                    V.scalar_tensor_tensor(dst[:, h], xi_pad[:, h, tap:tap + L], cw[:, h, tap:tap + 1], src[:, h],
                                           ALU.mult, ALU.add).then_inc(conv_step, 1)
                    src, dst = dst, src

            def times_up(b, j):
                n = TILES * b + j
                rows = SHARED[j] if j < NSH else P
                dve.wait_ge(silu_ready, n + 1)
                dve.wait_ge(up_ps, n + 1)
                if begun(n + 1 - AR if j >= AR else TILES * b):
                    dve.wait_ge(down_done, n + 1 - AR if j >= AR else TILES * b)
                V.tensor_tensor(act[0:rows, j % AR], silu_g[0:rows, j % 2], u_ps[0:rows, j % 2],
                                ALU.mult).then_inc(act_ready, 1)

            def router(b, steps=[0]):
                count = 0

                def step(instruction):
                    nonlocal count
                    count += 1
                    instruction.then_inc(rt_step, 1)
                    dve.wait_ge(rt_step, RT_STEPS * b + count)

                over = lambda ap: ap.unsqueeze(2).broadcast_to([P, NQ, NE])
                dve.wait_ge(lg_ps, b + 1)
                logits = misc_bank[:, 0:NQ * NE].rearrange("p (q e) -> p q e", e=NE)
                step(V.tensor_reduce(r_max[:], logits, AX.X, ALU.max))
                V.tensor_tensor(r_sh[:], logits, over(r_max[:]), ALU.subtract).then_inc(lg_taken, 1)
                yield
                dve.wait_ge(rex_ready, b + 1)
                step(V.tensor_reduce(r_sum[:], r_ex[:], AX.X, ALU.add))
                step(V.reciprocal(r_inv[:], r_sum[:]))
                step(V.tensor_tensor(r_sc[:], r_ex[:], over(r_inv[:]), ALU.mult))
                other = r_sc[:].unsqueeze(2).broadcast_to([P, NQ, NE, NE])
                own = r_sc[:].unsqueeze(3).broadcast_to([P, NQ, NE, NE])
                step(V.tensor_tensor(r_gt[:], other, own, ALU.is_gt))
                step(V.tensor_tensor(r_eq[:], other, own, ALU.is_equal))
                step(V.tensor_tensor(r_eq[:], r_eq[:], lower[:], ALU.mult))
                step(V.tensor_tensor(r_gt[:], r_gt[:], r_eq[:], ALU.add))
                step(V.tensor_reduce(r_rank[:], r_gt[:], AX.X, ALU.add))
                step(V.scalar_tensor_tensor(r_top[:], r_rank[:], 2.0, r_sc[:], ALU.is_lt, ALU.mult))
                step(V.tensor_reduce(r_den[:], r_top[:], AX.X, ALU.add))
                step(V.tensor_scalar(r_den[:], r_den[:], 1e-20, None, ALU.add))
                step(V.reciprocal(r_rden[:], r_den[:]))
                assert count == RT_STEPS
                V.tensor_tensor(w_tok[:].rearrange("p q (e r) -> p q e r", e=NE),
                                r_top[:].unsqueeze(3).broadcast_to([P, NQ, NE, QE]),
                                r_rden[:].unsqueeze(2).unsqueeze(3).broadcast_to([P, NQ, NE, QE]),
                                ALU.mult).then_inc(w_ready, 1)
                yield

            def iteration(i, doA, doS, doO, doG):
                a, o, g = i + 1, i - 1, i - 2
                if doA:
                    dve.wait_ge(xln_loaded, 16 * (a + 1))
                    stats(xln, stA, mvA, rsA, lnA_step, varA_ready, a)
                if doS:
                    scan(i, 0)
                if doO:
                    dve.wait_ge(sum_done, UNITS * i)
                    dve.wait_ge(z_ready, 2 * i)
                    if begun(NH * o):
                        dve.wait_ge(yT_ps, NH * o)
                    V.tensor_tensor(yg[:], y_ps[:], zg[:], ALU.mult).then_inc(yg_ready, 1)
                if doS:
                    times_c(i, 0)
                if doA:
                    dve.wait_ge(rsA_ready, a + 1)
                    if begun(a):
                        dve.wait_ge(xnT_ps, a)
                    normalize(xn, xln, mvA, rsA, xn_ready)
                if doG:
                    times_up(g, 7)
                if doS:
                    scan(i, 1)
                if doG:
                    times_up(g, 8)
                if doS:
                    times_c(i, 1)
                if doG:
                    times_up(g, 9)
                if doO:
                    dve.wait_ge(o_ready, o + 1)
                    stats(o_sb, stO, mvO, rsO, lnO_step, varO_ready, o)
                if doA:
                    conv(a, 0)
                if doG:
                    times_up(g, 10)
                if doS:
                    scan(i, 2)
                if doA:
                    conv(a, 1)
                if doG:
                    times_up(g, 11)
                if doO:
                    dve.wait_ge(rsO_ready, o + 1)
                    dve.wait_ge(xres_loaded, 16 * (o + 1))
                    if begun(16 * o):
                        dve.wait_ge(x1_moved, 16 * o)
                    normalize(o_sb, o_sb, mvO, rsO, on_ready)
                    dve.wait_ge(on_ready, NQ * (o + 1))
                    V.tensor_tensor(x1[:], o_sb[:], xres[:], ALU.add).then_inc(x1_ready, 1)
                    dve.wait_ge(x1_ready, o + 1)
                    stats(x1, st2, mv2, rs2, ln2_step, var2_ready, o)
                if doS:
                    times_c(i, 2)
                if doG:
                    times_up(g, 12)
                if doS:
                    scan(i, 3)
                if doG:
                    times_up(g, 13)
                if doO:
                    dve.wait_ge(rs2_ready, o + 1)
                    if begun(o):
                        dve.wait_ge(x1T_ps, o)
                    normalize(x1n, x1, mv2, rs2, x1n_ready)
                if doS:
                    times_c(i, 3)
                    scan(i, 4)
                if doG:
                    dve.wait_ge(down_done, TILES * (g + 1))
                    stats(f_ps, stG, mvG, rsG, lnG_step, varG_ready, g)
                route = router(o) if doO else None
                if doO:
                    next(route)
                if doS:
                    times_c(i, 4)
                if doA:
                    dve.wait_ge(sp_ready, a + 1)
                    if begun(UNITS * a):
                        dve.wait_ge(dA_ready, UNITS * a)
                    V.scalar_tensor_tensor(conv0[:], conv0[:], -1.0, sp_t[:], ALU.add, ALU.subtract).then_inc(dt_step, 1)
                    dve.wait_ge(dt_step, DT_STEPS * a + 1)
                    V.tensor_tensor(conv1[:], conv1[:], conv0[:], ALU.subtract).then_inc(dt_step, 1)
                    dve.wait_ge(dt_step, DT_STEPS * a + 2)
                    if begun(a):
                        dve.wait_ge(u_ready, a)
                    V.tensor_tensor(dt[:], conv1[:], sp_r[:], ALU.add).then_inc(dt_ready, 1)
                if doO:
                    next(route)
                    times_up(o, 0)
                if doS:
                    scan(i, 5)
                if doG:
                    dve.wait_ge(rsG_ready, g + 1)
                    dve.wait_ge(y_stored, 16 * g)
                    normalize(y_out, f_ps, mvG, rsG, f_taken)
                    dve.wait_ge(f_taken, NQ * (g + 1))
                    dve.wait_ge(x1_moved, 16 * (g + 1))
                    V.tensor_tensor(y_out[:], y_out[:], x1_old[:], ALU.add).then_inc(y_ready, 1)
                if doO:
                    times_up(o, 1)
                if doS:
                    times_c(i, 5)
                if doO:
                    times_up(o, 2)
                if doS:
                    scan(i, 6)
                if doO:
                    times_up(o, 3)
                if doS:
                    times_c(i, 6)
                if doO:
                    times_up(o, 4)
                if doS:
                    scan(i, 7)
                if doO:
                    times_up(o, 5)
                if doS:
                    times_c(i, 7)
                if doO:
                    times_up(o, 6)

            run(dve, iteration)

        @block.tensor
        def _(pe):
            T = nc.tensor

            misc = {
                "yT0": (2, yT_ready, NH, 1), "yT1": (2, yT_ready, NH, 2),
                "z0": (1, z_ready, 2, 1), "z1": (1, z_ready, 2, 2),
                "o": (2, o_ready, 1, 1),
                "xnT": (0, xnT_ready, 1, 1), "xi0": (0, xi_ready, NH, 1), "xi1": (0, xi_ready, NH, 2),
                "xp": (0, xp_ready, 1, 1),
                "x1T": (2, x1T_ready, 1, 1),
                "dt0": (0, dt_taken, NH, 1), "dt1": (0, dt_taken, NH, 2),
                "lg": (2, lg_taken, 1, 1), "wf": (2, wf_ready, 1, 1),
            }
            order = list(misc)

            def misc_free(name, i, stages):
                before = stages if not isinstance(i, int) else plan(i - 1)
                at = order.index(name)
                ran = [(n, i) for n in order[:at] if stages[misc[n][0]]]
                ran = ran or [(n, i - 1) for n in order if before[misc[n][0]]]
                if ran:
                    n, j = ran[-1]
                    stage, taken, per, count = misc[n]
                    b = j + 1 - stage
                    if begun(per * b + count):
                        pe.wait_ge(taken, per * b + count)

            def transposed(src, dst, done):
                for q in range(NQ):
                    last = T.transpose(dst[:, P * q:P * q + P], src(q), ident[:])
                last.then_inc(done, 1)

            def tile(b, j):
                n = TILES * b + j
                if j < NSH:
                    rows = SHARED[j]
                    wg_j, wu_j = s_gate[:, P * j:P * j + rows], s_up[:, P * j:P * j + rows]
                else:
                    rows = P
                    wg_j, wu_j = w_gate[:, :, j - NSH], w_up[:, :, j - NSH]
                if j == 0:
                    pe.wait_ge(x1T_ready, b + 1)
                if begun(n - 1):
                    pe.wait_ge(silu_ready, n - 1)
                T.matmul(g_ps[0:rows, j % 2], wg_j, x1T[:], start=True, stop=True).then_inc(gate_ps, 1)
                if begun(n - 1):
                    pe.wait_ge(act_ready, n - 1)
                T.matmul(u_ps[0:rows, j % 2], wu_j, x1T[:], start=True, stop=True).then_inc(up_ps, 1)

            def down(b, j):
                if j == 0:
                    if begun(NQ * b):
                        pe.wait_ge(f_taken, NQ * b)
                if j < NSH:
                    rows, w = SHARED[j], s_down[0:SHARED[j], j]
                    pe.wait_ge(act_ready, TILES * b + j + 1)
                else:
                    rows, w = P, w_down[:, j - NSH]
                    pe.wait_ge(actw_ready, ROUTED * b + j - NSH + 1)
                for q in range(NQ):
                    last = T.matmul(f_ps[:, q], act[0:rows, j % AR, P * q:P * q + P], w,
                                    start=(j == 0 and q == 0), stop=(j == TILES - 1), skip_group_check=True)
                last.then_inc(down_done, 1)

            def sum_unit(b, k):
                pe.wait_ge(hc_ready, UNITS * b + k + 1)
                h = k % NH
                for s in range(GS):
                    for q in range(NQ):
                        last = T.matmul(y_ps[:, q, P * h:P * h + P], hb[:, k % RING, s, P * q:P * q + P], ident[:],
                                        start=False, stop=(k >= UNITS - NH and s == GS - 1), is_transpose=True,
                                        skip_group_check=True)
                last.then_inc(sum_done, 1)

            def start_y(b):
                pe.wait_ge(xcD_ready, NH * (b + 1))
                if begun(b):
                    pe.wait_ge(yg_ready, b)
                for h in range(NH):
                    for q in range(NQ):
                        T.matmul(y_ps[:, q, P * h:P * h + P], xcD[:, h, P * q:P * q + P], ident[:],
                                 start=(h == 0 and q % 2 == 0), stop=False, is_transpose=True, skip_group_check=True)

            pe.wait_ge(const_ready, 2)
            pe.wait_ge(early_loaded, 16 * EARLY)

            def iteration(i, doA, doS, doO, doG):
                a, o, g = i + 1, i - 1, i - 2
                stages = (doA, doS, doO, doG)
                if doG:
                    tile(g, 7)
                    down(g, 4)
                if doO:
                    for h in range(NH):
                        pe.wait_ge(yg_ready, o + 1)
                        misc_free(f"yT{h}", i, stages)
                        transposed(lambda q: yg[:, q, P * h:P * h + P], misc_bank, yT_ps)
                if doS:
                    pe.wait_ge(xnT_ready, i + 1)
                    start_y(i)
                    for m in range(2):
                        misc_free(f"z{m}", i, stages)
                        for q in range(2):
                            last = T.matmul(misc_bank[:, DI * q:DI * q + DI], xnT[:, P * (2 * m + q):P * (2 * m + q + 1)],
                                            w_in[:, DI:2 * DI], start=True, stop=True)
                        last.then_inc(z_ps, 1)
                if doO:
                    misc_free("o", i, stages)
                    pe.wait_ge(yT_ready, NH * (o + 1))
                    for q in range(NQ):
                        for h in range(NH):
                            last = T.matmul(misc_bank[:, DM * q:DM * q + DM], ygT[:, h, P * q:P * q + P], w_out[:, h],
                                            start=(h == 0), stop=(h == NH - 1))
                    last.then_inc(o_ps, 1)
                if doG:
                    tile(g, 8)
                    down(g, 5)
                if doS:
                    sum_unit(i, 0)
                if doA:
                    pe.wait_ge(xn_ready, NQ * (a + 1))
                    misc_free("xnT", i, stages)
                    transposed(lambda q: xn[:, q], misc_bank, xnT_ps)
                if doG:
                    tile(g, 9)
                    down(g, 6)
                for h in range(NH):
                    if doA:
                        pe.wait_ge(xnT_ready, a + 1)
                        misc_free(f"xi{h}", i, stages)
                        T.matmul(misc_bank[:], w_in[:, P * h:P * h + P], xnT[:], start=True, stop=True).then_inc(xi_ps, 1)
                    if h == 0 and doG:
                        tile(g, 10)
                        down(g, 7)
                if doS:
                    sum_unit(i, 1)
                if doG:
                    tile(g, 11)
                    down(g, 8)
                    tile(g, 12)
                    down(g, 9)
                if doS:
                    sum_unit(i, 2)
                if doG:
                    tile(g, 13)
                    down(g, 10)
                if doA:
                    pe.wait_ge(xc_ready, NH * (a + 1))
                    misc_free("xp", i, stages)
                    for h in range(NH):
                        last = T.matmul(misc_bank[0:XP, :], w_x[:, h], xc[:, h], start=(h == 0), stop=(h == NH - 1))
                    last.then_inc(xp_ps, 1)
                if doO:
                    pe.wait_ge(x1n_ready, NQ * (o + 1))
                    misc_free("x1T", i, stages)
                    transposed(lambda q: x1n[:, q], misc_bank, x1T_ps)
                if doS:
                    sum_unit(i, 3)
                if doG:
                    for j in range(TILES - LAG, TILES):
                        down(g, j)
                if doA:
                    pe.wait_ge(xp_ready, a + 1)
                    for h in range(NH):
                        misc_free(f"dt{h}", i, stages)
                        T.matmul(misc_bank[:], w_dt[:, P * h:P * h + P], xproj[0:DR, :], start=True,
                                 stop=True).then_inc(dt_ps, 1)
                if doO:
                    if isinstance(i, int) and i == 1:
                        pe.wait_ge(late_loaded, 16 * LATE)
                    pe.wait_ge(x1T_ready, o + 1)
                    misc_free("lg", i, stages)
                    for q in range(NQ):
                        last = T.matmul(misc_bank[:, NE * q:NE * q + NE], x1T[:, P * q:P * q + P], gate[:],
                                        start=True, stop=True)
                    last.then_inc(lg_ps, 1)
                    tile(o, 0)
                if doS:
                    sum_unit(i, 4)
                if doO:
                    tile(o, 1)
                    pe.wait_ge(w_ready, o + 1)
                    misc_free("wf", i, stages)
                    for q in range(NQ):
                        last = T.matmul(misc_bank[:, P * q:P * q + P],
                                        w_tok[:, q], ident[:],
                                        start=True, stop=True, is_transpose=True)
                    last.then_inc(wf_ps, 1)
                    tile(o, 2)
                if doS:
                    sum_unit(i, 5)
                if doO:
                    tile(o, 3)
                    down(o, 0)
                    tile(o, 4)
                    down(o, 1)
                if doS:
                    sum_unit(i, 6)
                if doO:
                    tile(o, 5)
                    down(o, 2)
                    tile(o, 6)
                    down(o, 3)
                if doS:
                    sum_unit(i, 7)

            run(pe, iteration)


_INS = ["L0_attn_x", "L0_attn_W_in", "L0_attn_conv_w", "L0_attn_conv_b", "L0_attn_W_x", "L0_attn_W_dt",
        "L0_attn_b_dt", "L0_attn_A_log", "L0_attn_D", "L0_attn_W_out", "L0_ffn_gate_w", "L0_ffn_wg",
        "L0_ffn_wu", "L0_ffn_wd", "L0_ffn_swg", "L0_ffn_swu", "L0_ffn_swd"]
_OUTS = [((8, 512, 128), "float32")]


def kernel(**inputs):
    import numpy as _np
    import concourse.bacc as _bacc
    from concourse import mybir as _mybir
    from concourse.bass_utils import run_bass_kernel_spmd as _run

    nc = _bacc.Bacc("TRN2", target_bir_lowering=False, num_devices=1)
    arrays, args = {}, []
    for name in _INS:
        a = _np.ascontiguousarray(inputs[name])
        arrays[f"in_{name}_dram"] = a
        args.append(nc.dram_tensor(f"in_{name}_dram", a.shape, _mybir.dt.from_np(a.dtype), kind="ExternalInput").ap())
    for i, (shape, dtype) in enumerate(_OUTS):
        dt = _mybir.dt.from_np(_np.dtype(dtype))
        args.append(nc.dram_tensor(f"out_{i}_dram", shape, dt, kind="ExternalOutput").ap())
    layer_kernel(nc, *args)
    r = _run(nc, [arrays], core_ids=[0])
    got = tuple(r.results[0][f"out_{i}_dram"] for i in range(len(_OUTS)))
    return got[0]
```

```python
import concourse.bass as bass
from concourse import mybir
from contextlib import ExitStack

F32 = mybir.dt.float32
ALU = mybir.AluOpType
ACT = mybir.ActivationFunctionType
AX = mybir.AxisListType


def begun(value):
    return not isinstance(value, int) or value > 0


def layer_kernel(nc, x, W_in, conv_w, conv_b, W_x, W_dt, b_dt, A_log, D, W_out,
                 gate_w, wg, wu, wd, swg, swu, swd, out):
    P = 128
    NB, L, DM = x.shape
    DI = conv_w.shape[0]
    NH = DI // P
    TAPS = conv_w.shape[2]
    NS = A_log.shape[1]
    DR = W_dt.shape[0]
    XP = DR + 2 * NS
    NE, _, FE = wg.shape
    FS = swg.shape[1]
    NQ = L // P
    GS = 4
    NG = NS // GS
    UNITS = NG * NH
    RING = 4
    BC = 2
    QE = P // NE
    SHARED = [min(P, FS - P * j) for j in range((FS + P - 1) // P)]
    NSH = len(SHARED)
    TILES = NSH + FE // QE
    ROUTED = TILES - NSH
    AR = 5
    EPS = 1e-5
    assert DM == P and UNITS % RING == 0 and NG % BC == 0 and TILES % 2 == 0
    assert FE == ROUTED * QE and NH == 2 and NQ == 4

    with ExitStack() as ctx:
        def sb(name, shape, dtype=F32):
            return ctx.enter_context(nc.sbuf_tensor(name, shape, dtype))

        def psum(name, shape):
            return ctx.enter_context(nc.psum_tensor(name, shape, F32))

        def sem(name):
            return ctx.enter_context(nc.semaphore(name))

        w_in = sb("w_in", [P, 2 * DI])
        w_x = sb("w_x", [P, NH, XP])
        w_dt = sb("w_dt", [DR, DI])
        w_out = sb("w_out", [P, NH, DM])
        cw = sb("cw", [P, NH, TAPS])
        cb = sb("cb", [P, NH])
        bdt = sb("bdt", [P, NH])
        a_neg = sb("a_neg", [P, NH, NS])
        a_exp = sb("a_exp", [P, NH, NS])
        d_skip = sb("d_skip", [P, NH])
        gate = sb("gate", [P, NE])
        w_gate = sb("w_gate", [P, P, ROUTED])
        w_up = sb("w_up", [P, P, ROUTED])
        w_down = sb("w_down", [P, ROUTED, DM])
        s_gate = sb("s_gate", [P, FS])
        s_up = sb("s_up", [P, FS])
        s_down = sb("s_down", [P, NSH, DM])
        ident = sb("ident", [P, P])
        lower = sb("lower", [P, NQ, NE, NE])
        neg_half = sb("neg_half", [P, NQ])
        waited = sb("waited", [P, 1])
        xln = sb("xln", [P, NQ, DM])
        xn = sb("xn", [P, NQ, DM])
        xnT = sb("xnT", [P, L])
        stA = sb("stA", [P, NQ, 6])
        mvA = sb("mvA", [P, NQ, 2])
        rsA = sb("rsA", [P, NQ])
        nmA = sb("nmA", [P, NQ])
        xi_pad = sb("xi_pad", [P, NH, L + TAPS - 1])
        conv0 = sb("conv0", [P, NH, L])
        conv1 = sb("conv1", [P, NH, L])
        xc = sb("xc", [P, NH, L])
        xcD = sb("xcD", [P, NH, L])
        xproj = sb("xproj", [XP, L])
        dt = sb("dt", [P, NH, L])
        u = sb("u", [P, NH, L])
        dA = sb("dA", [P, RING, GS, L])
        hb = sb("hb", [P, RING, GS, L])
        b_all = sb("b_all", [P, BC, GS, L])
        c_all = sb("c_all", [P, BC, GS, L])
        zg = sb("zg", [P, NQ, DI])
        yg = sb("yg", [P, NQ, DI])
        ygT = sb("ygT", [P, NH, L])
        sp_r = yg[:].rearrange("p q d -> p (q d)").rearrange("p (h l) -> p h l", h=NH)
        sp_t = ygT
        xres = sb("xres", [P, NQ, DM])
        o_sb = sb("o_sb", [P, NQ, DM])
        stO = sb("stO", [P, NQ, 6])
        mvO = sb("mvO", [P, NQ, 2])
        rsO = sb("rsO", [P, NQ])
        nmO = sb("nmO", [P, NQ])
        st2 = sb("st2", [P, NQ, 6])
        mv2 = sb("mv2", [P, NQ, 2])
        rs2 = sb("rs2", [P, NQ])
        nm2 = sb("nm2", [P, NQ])
        x1 = sb("x1", [P, NQ, DM])
        x1n = sb("x1n", [P, NQ, DM])
        x1T = sb("x1T", [P, L])
        r_max = sb("r_max", [P, NQ])
        r_sh = sb("r_sh", [P, NQ, NE])
        r_ex = sb("r_ex", [P, NQ, NE])
        r_sum = sb("r_sum", [P, NQ])
        r_inv = sb("r_inv", [P, NQ])
        r_sc = sb("r_sc", [P, NQ, NE])
        r_gt = sb("r_gt", [P, NQ, NE, NE])
        r_eq = sb("r_eq", [P, NQ, NE, NE])
        r_rank = sb("r_rank", [P, NQ, NE])
        r_top = sb("r_top", [P, NQ, NE])
        r_den = sb("r_den", [P, NQ])
        r_rden = sb("r_rden", [P, NQ])
        w_tok = sb("w_tok", [P, NQ, P])
        w_feat = sb("w_feat", [P, L])
        silu_g = sb("silu_g", [P, 2, L])
        act = sb("act", [P, AR, L])
        x1_old = sb("x1_old", [P, NQ, DM])
        stG = sb("stG", [P, NQ, 6])
        mvG = sb("mvG", [P, NQ, 2])
        rsG = sb("rsG", [P, NQ])
        nmG = sb("nmG", [P, NQ])
        y_out = sb("y_out", [P, NQ, DM])

        bc_dram = nc.dram_tensor("bc_dram", (NB, 2 * NS, L), F32, kind="Internal").ap()

        y_ps = psum("y_ps", [P, NQ, DI])
        misc_bank = psum("misc_bank", [P, L])
        g_ps = psum("g_ps", [P, 2, L])
        u_ps = psum("u_ps", [P, 2, L])
        f_ps = psum("f_ps", [P, NQ, DM])

        early_loaded, late_loaded = sem("early_loaded"), sem("late_loaded")
        xln_loaded, xres_loaded = sem("xln_loaded"), sem("xres_loaded")
        bc_stored, x1_moved, y_stored = sem("bc_stored"), sem("x1_moved"), sem("y_stored")
        b_loaded = [sem(f"b_loaded{g}") for g in range(BC)]
        c_loaded = [sem(f"c_loaded{g}") for g in range(BC)]
        const_step, const_ready, a_ready_exp, a_ready = sem("const_step"), sem("const_ready"), sem("a_ready_exp"), sem("a_ready")
        zeros_ready, waited_step = sem("zeros_ready"), sem("waited_step")
        lnA_step, varA_ready, rsA_ready, xn_ready = sem("lnA_step"), sem("varA_ready"), sem("rsA_ready"), sem("xn_ready")
        xnT_ps, xnT_ready = sem("xnT_ps"), sem("xnT_ready")
        xi_ps, xi_ready, conv_step = sem("xi_ps"), sem("xi_ready"), sem("conv_step")
        xc_ready, xcD_ready = sem("xc_ready"), sem("xcD_ready")
        xp_ps, xp_ready = sem("xp_ps"), sem("xp_ready")
        dt_ps, dt_taken, sp_step, sp_ready = sem("dt_ps"), sem("dt_taken"), sem("sp_step"), sem("sp_ready")
        sp_added, y_started, rmax_step = sem("sp_added"), sem("y_started"), sem("rmax_step")
        powA_done, powO_done, pow2_done, powG_done = sem("powA_done"), sem("powO_done"), sem("pow2_done"), sem("powG_done")
        dt_step, dt_ready, u_ready = sem("dt_step"), sem("dt_ready"), sem("u_ready")
        z_ps, z_ready = sem("z_ps"), sem("z_ready")
        dA_ready, bu_ready, scan_done, hc_ready, sum_done = (
            sem("dA_ready"), sem("bu_ready"), sem("scan_done"), sem("hc_ready"), sem("sum_done"))
        yg_ready, yT_ps, yT_ready, o_ps, o_ready = (
            sem("yg_ready"), sem("yT_ps"), sem("yT_ready"), sem("o_ps"), sem("o_ready"))
        lnO_step, varO_ready, rsO_ready, on_ready = sem("lnO_step"), sem("varO_ready"), sem("rsO_ready"), sem("on_ready")
        x1_ready = sem("x1_ready")
        ln2_step, var2_ready, rs2_ready, x1n_ready = sem("ln2_step"), sem("var2_ready"), sem("rs2_ready"), sem("x1n_ready")
        x1T_ps, x1T_ready, lg_ps, lg_taken = sem("x1T_ps"), sem("x1T_ready"), sem("lg_ps"), sem("lg_taken")
        rt_step, rex_ready, w_ready, wf_ps, wf_ready = (
            sem("rt_step"), sem("rex_ready"), sem("w_ready"), sem("wf_ps"), sem("wf_ready"))
        gate_ps, up_ps, silu_ready, act_ready, actw_ready, down_done = (
            sem("gate_ps"), sem("up_ps"), sem("silu_ready"), sem("act_ready"), sem("actw_ready"), sem("down_done"))
        lnG_step, varG_ready, rsG_ready, f_taken, y_ready = (
            sem("lnG_step"), sem("varG_ready"), sem("rsG_ready"), sem("f_taken"), sem("y_ready"))

        tokens = lambda ap: ap.rearrange("(q p) m -> p q m", p=P)
        halves = lambda ap: ap.rearrange("(h p) n -> p h n", p=P)

        LN_STEPS = 2 * NQ
        CONV_STEPS = NH * (TAPS - 1)
        RT_STEPS = 12
        EARLY, LATE = 10, 5 + NSH

        def live(b):
            return not isinstance(b, int) or 0 <= b < NB

        def run(engine, iteration):
            for i in range(-1, 3):
                iteration(i)
            with engine.Fori(3, NB - 1) as i:
                iteration(i)
            for i in range(NB - 1, NB + 2):
                iteration(i)

        block = ctx.enter_context(nc.Block())

        @block.sync
        def _(sp):
            def load_x(b, first=False):
                if not live(b) or (isinstance(b, int) and b == 0 and not first):
                    return
                if begun(b):
                    sp.wait_ge(xn_ready, b)
                sp.dma_start(xln[:], tokens(x[b])).then_inc(xln_loaded, 16)

            load_x(0, first=True)
            for to, of in ((w_in[:], W_in), (cw[:], conv_w.rearrange("(h p) o k -> p h (o k)", p=P)),
                           (cb[:], conv_b.rearrange("(h p) -> p h", p=P)),
                           (w_x[:], halves(W_x)), (w_dt[:], W_dt),
                           (bdt[:], b_dt.rearrange("(h p) -> p h", p=P)),
                           (d_skip[:], D.rearrange("(h p) -> p h", p=P)),
                           (a_exp[:], halves(A_log)),
                           (w_out[:], halves(W_out)),
                           (gate[:], gate_w.rearrange("e m -> m e"))):
                with nc.allow_non_contiguous_dma(reason="a few small vectors, once"):
                    sp.dma_start(to, of).then_inc(early_loaded, 16)
            sp.dma_start(w_gate[:].rearrange("p f j -> p (f j)").rearrange("p (e r) -> p e r", e=NE),
                         wg.rearrange("e m r -> m e r")).then_inc(late_loaded, 16)
            sp.dma_start(w_up[:].rearrange("p f j -> p (f j)").rearrange("p (e r) -> p e r", e=NE),
                         wu.rearrange("e m r -> m e r")).then_inc(late_loaded, 16)
            sp.dma_start(s_gate[:], swg).then_inc(late_loaded, 16)
            sp.dma_start(s_up[:], swu).then_inc(late_loaded, 16)
            for j, n in enumerate(SHARED):
                sp.dma_start(s_down[0:n, j, :], swd[P * j:P * j + n, :]).then_inc(late_loaded, 16)
            sp.dma_start(w_down[:], wd.rearrange("e r h -> (e r) h").rearrange("(p j) h -> p j h", p=P))\
              .then_inc(late_loaded, 16)

            def store_bc(b):
                if not live(b):
                    return
                sp.wait_ge(xp_ready, b + 1)
                sp.dma_start(bc_dram[b], xproj[DR:XP, :]).then_inc(bc_stored, 16)

            def load_b(b, g):
                if not live(b):
                    return
                if g == 0:
                    sp.wait_ge(bc_stored, 16 * (b + 1))
                if begun(UNITS * b + NH * (g - BC + 1)):
                    sp.wait_ge(bu_ready, UNITS * b + NH * (g - BC + 1))
                sp.dma_start(b_all[:, g % BC].rearrange("p s l -> p (s l)"),
                             bc_dram[b, GS * g:GS * g + GS, :].rearrange("s l -> (s l)").unsqueeze(0)
                             .broadcast_to([P, GS * L])).then_inc(b_loaded[g % BC], 16)

            def load_c(b, g):
                if not live(b):
                    return
                if g == 0:
                    sp.wait_ge(bc_stored, 16 * (b + 1))
                if begun(UNITS * b + NH * (g - BC + 1)):
                    sp.wait_ge(hc_ready, UNITS * b + NH * (g - BC + 1))
                sp.dma_start(c_all[:, g % BC].rearrange("p s l -> p (s l)"),
                             bc_dram[b, NS + GS * g:NS + GS * g + GS, :].rearrange("s l -> (s l)").unsqueeze(0)
                             .broadcast_to([P, GS * L])).then_inc(c_loaded[g % BC], 16)

            def load_xres(b):
                if not live(b):
                    return
                if begun(b):
                    sp.wait_ge(x1_ready, b)
                sp.dma_start(xres[:], tokens(x[b])).then_inc(xres_loaded, 16)

            def move_x1(b):
                if not live(b):
                    return
                sp.wait_ge(x1_ready, b + 1)
                sp.dma_start(x1_old[:], x1[:]).then_inc(x1_moved, 16)

            def store_y(b):
                if not live(b):
                    return
                sp.wait_ge(y_ready, b + 1)
                sp.dma_start(tokens(out[b]), y_out[:]).then_inc(y_stored, 16)

            def iteration(i):
                nxt, cur, old, older = i + 1, i, i - 1, i - 2
                load_xres(old)
                load_x(nxt)
                load_c(cur, 0)
                move_x1(older)
                load_b(cur, 2)
                load_c(cur, 1)
                load_c(cur, 2)
                load_b(cur, 3)
                load_c(cur, 3)
                store_bc(nxt)
                load_b(nxt, 0)
                store_y(older)
                load_b(nxt, 1)

            run(sp, iteration)
            sp.wait_ge(y_stored, 16 * NB)

        @block.gpsimd
        def _(pool):
            nc.gpsimd.memset(neg_half[:], -0.5).then_inc(const_step, 1)
            nc.gpsimd.memset(ident[:], 0.0).then_inc(const_step, 1)
            nc.gpsimd.memset(lower[:], 1.0).then_inc(const_step, 1)
            pool.wait_ge(const_step, 3)
            nc.gpsimd.affine_select(out=ident[:], in_=ident[:], compare_op=ALU.not_equal, fill=1.0, base=0,
                                    pattern=[[-1, P]], channel_multiplier=1).then_inc(const_ready, 1)
            nc.gpsimd.affine_select(out=lower[:], in_=lower[:], compare_op=ALU.is_gt, fill=0.0, base=0,
                                    pattern=[[0, NQ], [1, NE], [-1, NE]], channel_multiplier=0).then_inc(const_ready, 1)

            def scales(b, rs, nm, var_ready, pow_done, rs_ready):
                if not live(b):
                    return
                pool.wait_ge(var_ready, b + 1)
                nc.gpsimd.tensor_tensor(rs[:], rs[:], neg_half[:], ALU.pow).then_inc(pow_done, 1)
                pool.wait_ge(pow_done, b + 1)
                nc.gpsimd.tensor_tensor(nm[:], nm[:], rs[:], ALU.mult).then_inc(rs_ready, 1)

            def scales_x(b):
                scales(b, rsA, nmA, varA_ready, powA_done, rsA_ready)

            def scales_o(b):
                scales(b, rsO, nmO, varO_ready, powO_done, rsO_ready)

            def scales_x1(b):
                scales(b, rs2, nm2, var2_ready, pow2_done, rs2_ready)

            def scales_f(b):
                scales(b, rsG, nmG, varG_ready, powG_done, rsG_ready)

            def add_relu(b):
                if not live(b):
                    return
                pool.wait_ge(sp_ready, b + 1)
                nc.gpsimd.tensor_tensor(conv1[:], conv1[:], sp_r[:], ALU.add).then_inc(sp_added, 1)

            def make_u(b):
                if not live(b):
                    return
                pool.wait_ge(dt_ready, b + 1)
                pool.wait_ge(xc_ready, NH * (b + 1))
                if begun(UNITS * b):
                    pool.wait_ge(bu_ready, UNITS * b)
                nc.gpsimd.tensor_tensor(u[:], dt[:], xc[:], ALU.mult).then_inc(u_ready, 1)

            def bu(b, k):
                if not live(b):
                    return
                g, h = k // NH, k % NH
                if k == 0:
                    pool.wait_ge(u_ready, b + 1)
                if h == 0:
                    pool.wait_ge(b_loaded[g % BC], 16 * (NG // BC * b + g // BC + 1))
                if begun(UNITS * b + k + 1 - RING):
                    pool.wait_ge(sum_done, UNITS * b + k + 1 - RING)
                nc.gpsimd.tensor_tensor(hb[:, k % RING], u[:, h, :].unsqueeze(1).broadcast_to([P, GS, L]),
                                        b_all[:, g % BC], ALU.mult).then_inc(bu_ready, 1)

            def weigh(b, j):
                if not live(b):
                    return
                pool.wait_ge(act_ready, TILES * b + j + 1)
                if j == NSH:
                    pool.wait_ge(wf_ready, b + 1)
                nc.gpsimd.tensor_tensor(act[:, j % AR], act[:, j % AR], w_feat[:], ALU.mult).then_inc(actw_ready, 1)

            def iteration(i):
                nxt, cur, old, older = i + 1, i, i - 1, i - 2
                bu(old, 6)
                bu(old, 7)
                add_relu(cur)
                weigh(older, 3)
                make_u(cur)
                bu(cur, 0)
                scales_x(nxt)
                weigh(older, 4)
                bu(cur, 1)
                weigh(older, 5)
                bu(cur, 2)
                weigh(older, 6)
                weigh(older, 7)
                scales_o(old)
                weigh(older, 8)
                weigh(older, 9)
                bu(cur, 3)
                weigh(older, 10)
                scales_x1(old)
                weigh(older, 11)
                bu(cur, 4)
                weigh(older, 12)
                weigh(older, 13)
                bu(cur, 5)
                scales_f(older)

            run(pool, iteration)

        @block.scalar
        def _(acte):
            A = nc.scalar
            acte.wait_ge(early_loaded, 16 * EARLY)
            A.activation(a_neg[:], a_exp[:], ACT.Exp).then_inc(a_ready_exp, 1)

            def normalize(dst, src, rs, nm, done):
                for q in range(NQ):
                    last = A.activation(dst[:, q], src[:, q], ACT.Identity, scale=rs[:, q:q + 1], bias=nm[:, q:q + 1])
                last.then_inc(done, 1)

            def normalize_x(b):
                if not live(b):
                    return
                acte.wait_ge(rsA_ready, b + 1)
                if begun(b):
                    acte.wait_ge(xnT_ps, b)
                normalize(xn, xln, rsA, nmA, xn_ready)

            def take_xnT(b):
                if not live(b):
                    return
                acte.wait_ge(xnT_ps, b + 1)
                if begun(NH * b):
                    acte.wait_ge(xi_ps, NH * b)
                if begun(2 * b):
                    acte.wait_ge(z_ps, 2 * b)
                A.copy(xnT[:], misc_bank[:]).then_inc(xnT_ready, 1)

            def take_xi(b, h):
                if not live(b):
                    return
                acte.wait_ge(xi_ps, NH * b + h + 1)
                if begun(b):
                    acte.wait_ge(dt_ready, b)
                A.activation(conv0[:, h], misc_bank[:], ACT.Identity, bias=cb[:, h:h + 1],
                             scale=cw[:, h, TAPS - 1:TAPS])
                A.copy(xi_pad[:, h, TAPS - 1:], misc_bank[:]).then_inc(xi_ready, 1)

            def silu_conv(b, h):
                if not live(b):
                    return
                acte.wait_ge(conv_step, CONV_STEPS * b + (TAPS - 1) * (h + 1))
                if begun(b):
                    acte.wait_ge(u_ready, b)
                if begun(b):
                    acte.wait_ge(xcD_ready, b)
                A.activation(xc[:, h], conv1[:, h], ACT.Silu).then_inc(xc_ready, 1)

            def skip(b):
                if not live(b):
                    return
                acte.wait_ge(xc_ready, NH * (b + 1))
                if begun(b):
                    acte.wait_ge(y_started, b)
                for h in range(NH):
                    last = A.activation(xcD[:, h], xc[:, h], ACT.Copy, scale=d_skip[:, h:h + 1])
                last.then_inc(xcD_ready, 1)

            def take_xproj(b):
                if not live(b):
                    return
                acte.wait_ge(xp_ps, b + 1)
                if begun(NH * b):
                    acte.wait_ge(dt_ps, NH * b)
                if begun(16 * b):
                    acte.wait_ge(bc_stored, 16 * b)
                A.copy(xproj[:], misc_bank[0:XP, :]).then_inc(xp_ready, 1)

            def take_dt(b, h):
                if not live(b):
                    return
                acte.wait_ge(dt_ps, NH * b + h + 1)
                if begun(b - 1):
                    acte.wait_ge(o_ps, b - 1)
                A.activation(sp_t[:, h], misc_bank[:], ACT.Abs, bias=bdt[:, h:h + 1])
                A.activation(sp_r[:, h], misc_bank[:], ACT.Relu, bias=bdt[:, h:h + 1]).then_inc(dt_taken, 1)

            def softplus_log(b):
                if not live(b):
                    return
                acte.wait_ge(dt_taken, NH * (b + 1))
                A.activation(sp_t[:], sp_t[:], ACT.Exp, scale=-1.0).then_inc(sp_step, 1)
                acte.wait_ge(sp_step, 2 * b + 1)
                A.activation(conv0[:], sp_t[:], ACT.Identity, bias=1.0).then_inc(sp_step, 1)
                acte.wait_ge(sp_step, 2 * b + 2)
                A.activation(conv1[:], conv0[:], ACT.Ln).then_inc(sp_ready, 1)

            def discount(b, k):
                if not live(b):
                    return
                g, h = k // NH, k % NH
                if begun(UNITS * b + k + 1 - RING):
                    acte.wait_ge(scan_done, UNITS * b + k + 1 - RING)
                if k == 0:
                    acte.wait_ge(dt_ready, b + 1)
                for s in range(GS):
                    last = A.activation(dA[:, k % RING, s, 1:L], dt[:, h, 1:L], ACT.Exp,
                                        scale=a_neg[:, h, GS * g + s:GS * g + s + 1])
                last.then_inc(dA_ready, 1)

            def silu_z(b, m):
                if not live(b):
                    return
                acte.wait_ge(z_ps, 2 * b + m + 1)
                if begun(b):
                    acte.wait_ge(yg_ready, b)
                A.activation(zg[:, 2 * m:2 * m + 2].rearrange("p q d -> p (q d)"), misc_bank[:],
                             ACT.Silu).then_inc(z_ready, 1)

            def take_yT(b, h):
                if not live(b):
                    return
                acte.wait_ge(yT_ps, NH * b + h + 1)
                if begun(b):
                    acte.wait_ge(o_ps, b)
                A.copy(ygT[:, h], misc_bank[:]).then_inc(yT_ready, 1)

            def take_o(b):
                if not live(b):
                    return
                acte.wait_ge(o_ps, b + 1)
                if begun(b):
                    acte.wait_ge(x1_ready, b)
                A.copy(o_sb[:].rearrange("p q m -> p (q m)"), misc_bank[:]).then_inc(o_ready, 1)

            def normalize_o(b):
                if not live(b):
                    return
                acte.wait_ge(rsO_ready, b + 1)
                normalize(o_sb, o_sb, rsO, nmO, on_ready)

            def normalize_x1(b):
                if not live(b):
                    return
                acte.wait_ge(rs2_ready, b + 1)
                if begun(b):
                    acte.wait_ge(x1T_ps, b)
                normalize(x1n, x1, rs2, nm2, x1n_ready)

            def take_x1T(b):
                if not live(b):
                    return
                acte.wait_ge(x1T_ps, b + 1)
                if begun(b):
                    acte.wait_ge(lg_ps, b)
                if begun(TILES * b):
                    acte.wait_ge(gate_ps, TILES * b)
                if begun(TILES * b):
                    acte.wait_ge(up_ps, TILES * b)
                A.copy(x1T[:], misc_bank[:]).then_inc(x1T_ready, 1)

            def router_exp(b):
                if not live(b):
                    return
                acte.wait_ge(lg_taken, b + 1)
                if begun(b):
                    acte.wait_ge(w_ready, b)
                A.activation(r_ex[:], r_sh[:], ACT.Exp).then_inc(rex_ready, 1)

            def take_w_feat(b):
                if not live(b):
                    return
                acte.wait_ge(wf_ps, b + 1)
                if begun(ROUTED * b):
                    acte.wait_ge(actw_ready, ROUTED * b)
                A.copy(w_feat[:], misc_bank[:]).then_inc(wf_ready, 1)

            def silu_tile(b, j):
                if not live(b):
                    return
                n = TILES * b + j
                rows = SHARED[j] if j < NSH else P
                acte.wait_ge(gate_ps, n + 1)
                if begun(n - 1):
                    acte.wait_ge(act_ready, n - 1)
                A.activation(silu_g[0:rows, j % 2], g_ps[0:rows, j % 2], ACT.Silu).then_inc(silu_ready, 1)

            def normalize_f(b):
                if not live(b):
                    return
                acte.wait_ge(rsG_ready, b + 1)
                if begun(16 * b):
                    acte.wait_ge(y_stored, 16 * b)
                normalize(y_out, f_ps, rsG, nmG, f_taken)

            def iteration(i):
                nxt, cur, old, older = i + 1, i, i - 1, i - 2
                silu_tile(older, 3)
                router_exp(older)
                take_dt(cur, 1)
                softplus_log(cur)
                discount(old, 7)
                silu_tile(older, 4)
                take_w_feat(older)
                silu_tile(older, 5)
                silu_tile(older, 6)
                discount(cur, 0)
                discount(cur, 1)
                discount(cur, 2)
                take_yT(old, 0)
                silu_tile(older, 7)
                take_yT(old, 1)
                silu_tile(older, 8)
                silu_z(cur, 0)
                silu_tile(older, 9)
                silu_z(cur, 1)
                normalize_x(nxt)
                take_o(old)
                silu_tile(older, 10)
                take_xnT(nxt)
                take_xi(nxt, 0)
                silu_tile(older, 11)
                normalize_o(old)
                take_xi(nxt, 1)
                discount(cur, 3)
                silu_tile(older, 12)
                silu_conv(nxt, 0)
                silu_tile(older, 13)
                silu_conv(nxt, 1)
                discount(cur, 4)
                normalize_x1(old)
                take_xproj(nxt)
                discount(cur, 5)
                take_x1T(old)
                discount(cur, 6)
                silu_tile(old, 0)
                normalize_f(older)
                silu_tile(old, 1)
                take_dt(nxt, 0)
                silu_tile(old, 2)
                skip(nxt)

            run(acte, iteration)

        @block.vector
        def _(dve):
            V = nc.vector
            V.memset(dA[:, :, :, 0:1], 0.0).then_inc(zeros_ready, 1)
            V.memset(xi_pad[:, :, 0:TAPS - 1], 0.0).then_inc(zeros_ready, 1)

            def stats(b, src, st, mv, rs, nm, step, ready):
                for q in range(NQ):
                    V.bn_stats(st[:, q], src[:, q]).then_inc(step, 1)
                dve.wait_ge(step, LN_STEPS * b + NQ)
                V.memset(waited[:], 0.0).then_inc(waited_step, 1)
                for q in range(NQ):
                    V.bn_aggr(mv[:, q], st[:, q]).then_inc(step, 1)
                dve.wait_ge(step, LN_STEPS * b + 2 * NQ)
                V.tensor_scalar(nm[:], mv[:, :, 0], -1.0, None, ALU.mult)
                V.tensor_scalar(rs[:], mv[:, :, 1], EPS, None, ALU.add).then_inc(ready, 1)

            def stats_x(b):
                if not live(b):
                    return
                dve.wait_ge(xln_loaded, 16 * (b + 1))
                if begun(b):
                    dve.wait_ge(xn_ready, b)
                stats(b, xln, stA, mvA, rsA, nmA, lnA_step, varA_ready)

            def stats_o(b):
                if not live(b):
                    return
                dve.wait_ge(o_ready, b + 1)
                stats(b, o_sb, stO, mvO, rsO, nmO, lnO_step, varO_ready)

            def stats_x1(b):
                if not live(b):
                    return
                dve.wait_ge(x1_ready, b + 1)
                stats(b, x1, st2, mv2, rs2, nm2, ln2_step, var2_ready)

            def stats_f(b):
                if not live(b):
                    return
                dve.wait_ge(down_done, TILES * (b + 1))
                stats(b, f_ps, stG, mvG, rsG, nmG, lnG_step, varG_ready)

            def conv(b, h):
                if not live(b):
                    return
                dve.wait_ge(xi_ready, NH * b + h + 1)
                src, dst = conv0, conv1
                for m, tap in enumerate(range(TAPS - 2, -1, -1)):
                    if m:
                        dve.wait_ge(conv_step, CONV_STEPS * b + (TAPS - 1) * h + m)
                    V.scalar_tensor_tensor(dst[:, h], xi_pad[:, h, tap:tap + L], cw[:, h, tap:tap + 1], src[:, h],
                                           ALU.mult, ALU.add).then_inc(conv_step, 1)
                    src, dst = dst, src

            def make_dt(b):
                if not live(b):
                    return
                dve.wait_ge(sp_ready, b + 1)
                V.scalar_tensor_tensor(conv0[:], conv0[:], -1.0, sp_t[:], ALU.add, ALU.subtract).then_inc(dt_step, 1)
                dve.wait_ge(dt_step, b + 1)
                dve.wait_ge(sp_added, b + 1)
                if begun(UNITS * b):
                    dve.wait_ge(dA_ready, UNITS * b)
                if begun(b):
                    dve.wait_ge(u_ready, b)
                V.tensor_tensor(dt[:], conv1[:], conv0[:], ALU.subtract).then_inc(dt_ready, 1)

            def scan(b, k):
                if not live(b):
                    return
                dve.wait_ge(dA_ready, UNITS * b + k + 1)
                dve.wait_ge(bu_ready, UNITS * b + k + 1)
                h_of = hb[:, k % RING].rearrange("p s l -> p (s l)")
                V.tensor_tensor_scan(h_of, dA[:, k % RING].rearrange("p s l -> p (s l)"), h_of, 0.0,
                                     ALU.mult, ALU.add).then_inc(scan_done, 1)

            def times_c(b, k):
                if not live(b):
                    return
                g = k // NH
                if k % NH == 0:
                    dve.wait_ge(c_loaded[g % BC], 16 * (NG // BC * b + g // BC + 1))
                dve.wait_ge(scan_done, UNITS * b + k + 1)
                V.tensor_tensor(hb[:, k % RING], hb[:, k % RING], c_all[:, g % BC], ALU.mult).then_inc(hc_ready, 1)

            def gate_y(b):
                if not live(b):
                    return
                dve.wait_ge(sum_done, UNITS * (b + 1))
                dve.wait_ge(z_ready, 2 * (b + 1))
                if begun(NH * b):
                    dve.wait_ge(yT_ps, NH * b)
                dve.wait_ge(dt_ready, min(b + 2, NB) if isinstance(b, int) else b + 2)
                V.tensor_tensor(yg[:], y_ps[:], zg[:], ALU.mult).then_inc(yg_ready, 1)

            def add_x(b):
                if not live(b):
                    return
                dve.wait_ge(on_ready, b + 1)
                dve.wait_ge(xres_loaded, 16 * (b + 1))
                if begun(b):
                    dve.wait_ge(x1n_ready, b)
                if begun(16 * b):
                    dve.wait_ge(x1_moved, 16 * b)
                V.tensor_tensor(x1[:], o_sb[:], xres[:], ALU.add).then_inc(x1_ready, 1)

            def router_max(b):
                if not live(b):
                    return
                over = lambda ap: ap.unsqueeze(2).broadcast_to([P, NQ, NE])
                dve.wait_ge(lg_ps, b + 1)
                logits = misc_bank[:, 0:NQ * NE].rearrange("p (q e) -> p q e", e=NE)
                V.tensor_reduce(r_max[:], logits, AX.X, ALU.max).then_inc(rmax_step, 1)
                dve.wait_ge(rmax_step, b + 1)
                V.tensor_tensor(r_sh[:], logits, over(r_max[:]), ALU.subtract).then_inc(lg_taken, 1)

            def router_weights(b):
                if not live(b):
                    return
                count = 0

                def step(instruction):
                    nonlocal count
                    count += 1
                    instruction.then_inc(rt_step, 1)

                over = lambda ap: ap.unsqueeze(2).broadcast_to([P, NQ, NE])
                dve.wait_ge(rex_ready, b + 1)
                step(V.tensor_reduce(r_sum[:], r_ex[:], AX.X, ALU.add))
                dve.wait_ge(rt_step, RT_STEPS * b + count)
                step(V.reciprocal(r_inv[:], r_sum[:]))
                dve.wait_ge(rt_step, RT_STEPS * b + count)
                step(V.tensor_tensor(r_sc[:], r_ex[:], over(r_inv[:]), ALU.mult))
                other = r_sc[:].unsqueeze(2).broadcast_to([P, NQ, NE, NE])
                own = r_sc[:].unsqueeze(3).broadcast_to([P, NQ, NE, NE])
                dve.wait_ge(rt_step, RT_STEPS * b + count)
                step(V.tensor_tensor(r_gt[:], other, own, ALU.is_gt))
                step(V.tensor_tensor(r_eq[:], other, own, ALU.is_equal))
                dve.wait_ge(rt_step, RT_STEPS * b + count)
                step(V.tensor_tensor(r_eq[:], r_eq[:], lower[:], ALU.mult))
                dve.wait_ge(rt_step, RT_STEPS * b + count)
                step(V.tensor_tensor(r_gt[:], r_gt[:], r_eq[:], ALU.add))
                dve.wait_ge(rt_step, RT_STEPS * b + count)
                step(V.tensor_reduce(r_rank[:], r_gt[:], AX.X, ALU.add))
                dve.wait_ge(rt_step, RT_STEPS * b + count)
                step(V.scalar_tensor_tensor(r_top[:], r_rank[:], 2.0, r_sc[:], ALU.is_lt, ALU.mult))
                dve.wait_ge(rt_step, RT_STEPS * b + count)
                step(V.tensor_reduce(r_den[:], r_top[:], AX.X, ALU.add))
                dve.wait_ge(rt_step, RT_STEPS * b + count)
                step(V.tensor_scalar(r_den[:], r_den[:], 1e-20, None, ALU.add))
                dve.wait_ge(rt_step, RT_STEPS * b + count)
                step(V.reciprocal(r_rden[:], r_den[:]))
                assert count == RT_STEPS
                dve.wait_ge(rt_step, RT_STEPS * b + count)
                if begun(b):
                    dve.wait_ge(wf_ps, b)
                V.tensor_tensor(w_tok[:].rearrange("p q (e r) -> p q e r", e=NE),
                                r_top[:].unsqueeze(3).broadcast_to([P, NQ, NE, QE]),
                                r_rden[:].unsqueeze(2).unsqueeze(3).broadcast_to([P, NQ, NE, QE]),
                                ALU.mult).then_inc(w_ready, 1)

            def times_up(b, j):
                if not live(b):
                    return
                n = TILES * b + j
                rows = SHARED[j] if j < NSH else P
                dve.wait_ge(silu_ready, n + 1)
                dve.wait_ge(up_ps, n + 1)
                last = j - AR if j >= AR else j + (TILES - 1 - j) // AR * AR - TILES
                if begun(TILES * b + last + 1):
                    dve.wait_ge(down_done, TILES * b + last + 1)
                V.tensor_tensor(act[0:rows, j % AR], silu_g[0:rows, j % 2], u_ps[0:rows, j % 2],
                                ALU.mult).then_inc(act_ready, 1)

            def add_x1(b):
                if not live(b):
                    return
                dve.wait_ge(f_taken, b + 1)
                dve.wait_ge(x1_moved, 16 * (b + 1))
                V.tensor_tensor(y_out[:], y_out[:], x1_old[:], ALU.add).then_inc(y_ready, 1)

            dve.wait_ge(a_ready_exp, 1)
            dve.wait_ge(zeros_ready, 2)
            V.tensor_scalar(a_neg[:], a_neg[:], -1.0, None, ALU.mult).then_inc(a_ready, 1)
            dve.wait_ge(a_ready, 1)
            dve.wait_ge(const_ready, 2)

            def iteration(i):
                nxt, cur, old, older = i + 1, i, i - 1, i - 2
                times_up(older, 1)
                scan(old, 6)
                times_up(older, 2)
                router_weights(older)
                times_up(older, 3)
                times_c(old, 6)
                make_dt(cur)
                times_up(older, 4)
                scan(old, 7)
                times_c(old, 7)
                stats_x(nxt)
                times_up(older, 5)
                times_up(older, 6)
                gate_y(old)
                scan(cur, 0)
                times_c(cur, 0)
                times_up(older, 7)
                times_up(older, 8)
                scan(cur, 1)
                times_c(cur, 1)
                times_up(older, 9)
                stats_o(old)
                scan(cur, 2)
                conv(nxt, 0)
                times_up(older, 10)
                add_x(old)
                conv(nxt, 1)
                stats_x1(old)
                times_up(older, 11)
                times_c(cur, 2)
                scan(cur, 3)
                times_up(older, 12)
                times_c(cur, 3)
                times_up(older, 13)
                scan(cur, 4)
                times_c(cur, 4)
                stats_f(older)
                scan(cur, 5)
                router_max(old)
                times_up(old, 0)
                times_c(cur, 5)
                add_x1(older)

            run(dve, iteration)

        @block.tensor
        def _(pe):
            T = nc.tensor

            misc = {
                "lg": (-2, lg_taken, 1, 1),
                "dt0": (0, dt_taken, NH, 1),
                "dt1": (0, dt_taken, NH, 2),
                "wf": (-2, wf_ready, 1, 1),
                "yT0": (-1, yT_ready, NH, 1),
                "yT1": (-1, yT_ready, NH, 2),
                "z0": (0, z_ready, 2, 1),
                "z1": (0, z_ready, 2, 2),
                "o": (-1, o_ready, 1, 1),
                "xnT": (1, xnT_ready, 1, 1),
                "xi0": (1, xi_ready, NH, 1),
                "xi1": (1, xi_ready, NH, 2),
                "xp": (1, xp_ready, 1, 1),
                "x1T": (-1, x1T_ready, 1, 1),
            }
            uses = list(misc)

            def misc_free(name, b):
                i, at = b - misc[name][0], uses.index(name)
                order = [(n, i - 1 + misc[n][0]) for n in uses] + [(n, i + misc[n][0]) for n in uses[:at]]
                order = [(n, before) for n, before in order if live(before)]
                if order:
                    n, before = order[-1]
                    _, taken, per_batch, count = misc[n]
                    pe.wait_ge(taken, per_batch * before + count)

            def transposed(src, dst, done):
                for q in range(NQ):
                    last = T.transpose(dst[:, P * q:P * q + P], src(q), ident[:])
                last.then_inc(done, 1)

            def transpose_xn(b):
                if not live(b):
                    return
                pe.wait_ge(xn_ready, b + 1)
                misc_free("xnT", b)
                transposed(lambda q: xn[:, q], misc_bank, xnT_ps)

            def project_xi(b, h):
                if not live(b):
                    return
                pe.wait_ge(xnT_ready, b + 1)
                misc_free(f"xi{h}", b)
                T.matmul(misc_bank[:], w_in[:, P * h:P * h + P], xnT[:], start=True, stop=True).then_inc(xi_ps, 1)

            def project_x(b):
                if not live(b):
                    return
                pe.wait_ge(xc_ready, NH * (b + 1))
                misc_free("xp", b)
                for h in range(NH):
                    last = T.matmul(misc_bank[0:XP, :], w_x[:, h], xc[:, h], start=(h == 0), stop=(h == NH - 1))
                last.then_inc(xp_ps, 1)

            def project_dt(b, h):
                if not live(b):
                    return
                pe.wait_ge(xp_ready, b + 1)
                misc_free(f"dt{h}", b)
                T.matmul(misc_bank[:], w_dt[:, P * h:P * h + P], xproj[0:DR, :], start=True,
                         stop=True).then_inc(dt_ps, 1)

            def start_y(b):
                if not live(b):
                    return
                pe.wait_ge(xcD_ready, b + 1)
                if begun(b):
                    pe.wait_ge(yg_ready, b)
                for h in range(NH):
                    for q in range(NQ):
                        last = T.matmul(y_ps[:, q, P * h:P * h + P], xcD[:, h, P * q:P * q + P], ident[:],
                                        start=(h == 0 and q % 2 == 0), stop=False, is_transpose=True,
                                        skip_group_check=True)
                last.then_inc(y_started, 1)

            def sum_unit(b, k):
                if not live(b):
                    return
                pe.wait_ge(hc_ready, UNITS * b + k + 1)
                h = k % NH
                for s in range(GS):
                    for q in range(NQ):
                        last = T.matmul(y_ps[:, q, P * h:P * h + P], hb[:, k % RING, s, P * q:P * q + P], ident[:],
                                        start=False, stop=(k >= UNITS - NH and s == GS - 1), is_transpose=True,
                                        skip_group_check=True)
                last.then_inc(sum_done, 1)

            def project_z(b, m):
                if not live(b):
                    return
                pe.wait_ge(xnT_ready, b + 1)
                misc_free(f"z{m}", b)
                for q in range(2):
                    last = T.matmul(misc_bank[:, DI * q:DI * q + DI], xnT[:, P * (2 * m + q):P * (2 * m + q + 1)],
                                    w_in[:, DI:2 * DI], start=True, stop=True)
                last.then_inc(z_ps, 1)

            def transpose_y(b, h):
                if not live(b):
                    return
                pe.wait_ge(yg_ready, b + 1)
                misc_free(f"yT{h}", b)
                transposed(lambda q: yg[:, q, P * h:P * h + P], misc_bank, yT_ps)

            def project_out(b):
                if not live(b):
                    return
                pe.wait_ge(yT_ready, NH * (b + 1))
                misc_free("o", b)
                for q in range(NQ):
                    for h in range(NH):
                        last = T.matmul(misc_bank[:, DM * q:DM * q + DM], ygT[:, h, P * q:P * q + P], w_out[:, h],
                                        start=(h == 0), stop=(h == NH - 1))
                last.then_inc(o_ps, 1)

            def transpose_x1(b):
                if not live(b):
                    return
                pe.wait_ge(x1n_ready, b + 1)
                misc_free("x1T", b)
                transposed(lambda q: x1n[:, q], misc_bank, x1T_ps)

            def logits(b):
                if not live(b):
                    return
                pe.wait_ge(x1T_ready, b + 1)
                misc_free("lg", b)
                for q in range(NQ):
                    last = T.matmul(misc_bank[:, NE * q:NE * q + NE], x1T[:, P * q:P * q + P], gate[:],
                                    start=True, stop=True)
                last.then_inc(lg_ps, 1)

            def transpose_w(b):
                if not live(b):
                    return
                pe.wait_ge(w_ready, b + 1)
                misc_free("wf", b)
                for q in range(NQ):
                    last = T.matmul(misc_bank[:, P * q:P * q + P], w_tok[:, q], ident[:],
                                    start=True, stop=True, is_transpose=True)
                last.then_inc(wf_ps, 1)

            def gate_tile(b, j):
                if not live(b):
                    return
                rows = SHARED[j] if j < NSH else P
                w = s_gate[:, P * j:P * j + rows] if j < NSH else w_gate[:, :, j - NSH]
                if j == 0:
                    pe.wait_ge(x1T_ready, b + 1)
                    if isinstance(b, int) and b == 0:
                        pe.wait_ge(late_loaded, 16 * LATE)
                if begun(TILES * b + j - 1):
                    pe.wait_ge(silu_ready, TILES * b + j - 1)
                T.matmul(g_ps[0:rows, j % 2], w, x1T[:], start=True, stop=True).then_inc(gate_ps, 1)

            def up_tile(b, j):
                if not live(b):
                    return
                rows = SHARED[j] if j < NSH else P
                w = s_up[:, P * j:P * j + rows] if j < NSH else w_up[:, :, j - NSH]
                if begun(TILES * b + j - 1):
                    pe.wait_ge(act_ready, TILES * b + j - 1)
                T.matmul(u_ps[0:rows, j % 2], w, x1T[:], start=True, stop=True).then_inc(up_ps, 1)

            def down(b, j):
                if not live(b):
                    return
                if j == 0:
                    if begun(b):
                        pe.wait_ge(f_taken, b)
                if j < NSH:
                    rows, w = SHARED[j], s_down[0:SHARED[j], j]
                    pe.wait_ge(act_ready, TILES * b + j + 1)
                else:
                    rows, w = P, w_down[:, j - NSH]
                    pe.wait_ge(actw_ready, ROUTED * b + j - NSH + 1)
                for q in range(NQ):
                    last = T.matmul(f_ps[:, q], act[0:rows, j % AR, P * q:P * q + P], w,
                                    start=(j == 0 and q == 0), stop=(j == TILES - 1), skip_group_check=True)
                last.then_inc(down_done, 1)

            pe.wait_ge(const_ready, 2)
            pe.wait_ge(early_loaded, 16 * EARLY)

            def iteration(i):
                nxt, cur, old, older = i + 1, i, i - 1, i - 2
                gate_tile(older, 0)
                logits(older)
                up_tile(older, 0)
                gate_tile(older, 1)
                project_dt(cur, 0)
                gate_tile(older, 2)
                up_tile(older, 1)
                gate_tile(older, 3)
                up_tile(older, 2)
                project_dt(cur, 1)
                gate_tile(older, 4)
                down(older, 0)
                sum_unit(old, 4)
                down(older, 1)
                up_tile(older, 3)
                gate_tile(older, 5)
                up_tile(older, 4)
                down(older, 2)
                sum_unit(old, 5)
                transpose_w(older)
                gate_tile(older, 6)
                up_tile(older, 5)
                gate_tile(older, 7)
                up_tile(older, 6)
                sum_unit(old, 6)
                gate_tile(older, 8)
                sum_unit(old, 7)
                up_tile(older, 7)
                down(older, 3)
                transpose_y(old, 0)
                up_tile(older, 8)
                down(older, 4)
                transpose_y(old, 1)
                start_y(cur)
                project_z(cur, 0)
                gate_tile(older, 9)
                project_z(cur, 1)
                up_tile(older, 9)
                project_out(old)
                gate_tile(older, 10)
                transpose_xn(nxt)
                down(older, 5)
                project_xi(nxt, 0)
                gate_tile(older, 11)
                down(older, 6)
                project_xi(nxt, 1)
                up_tile(older, 10)
                down(older, 7)
                up_tile(older, 11)
                gate_tile(older, 12)
                down(older, 8)
                up_tile(older, 12)
                down(older, 9)
                gate_tile(older, 13)
                sum_unit(cur, 0)
                up_tile(older, 13)
                down(older, 10)
                sum_unit(cur, 1)
                project_x(nxt)
                down(older, 11)
                sum_unit(cur, 2)
                down(older, 12)
                transpose_x1(old)
                down(older, 13)
                sum_unit(cur, 3)

            run(pe, iteration)


_INS = ["L0_attn_x", "L0_attn_W_in", "L0_attn_conv_w", "L0_attn_conv_b", "L0_attn_W_x", "L0_attn_W_dt",
        "L0_attn_b_dt", "L0_attn_A_log", "L0_attn_D", "L0_attn_W_out", "L0_ffn_gate_w", "L0_ffn_wg",
        "L0_ffn_wu", "L0_ffn_wd", "L0_ffn_swg", "L0_ffn_swu", "L0_ffn_swd"]
_OUTS = [((8, 512, 128), "float32")]


def kernel(**inputs):
    import numpy as _np
    import concourse.bacc as _bacc
    from concourse import mybir as _mybir
    from concourse.bass_utils import run_bass_kernel_spmd as _run

    nc = _bacc.Bacc("TRN2", target_bir_lowering=False, num_devices=1)
    arrays, args = {}, []
    for name in _INS:
        a = _np.ascontiguousarray(inputs[name])
        arrays[f"in_{name}_dram"] = a
        args.append(nc.dram_tensor(f"in_{name}_dram", a.shape, _mybir.dt.from_np(a.dtype), kind="ExternalInput").ap())
    for i, (shape, dtype) in enumerate(_OUTS):
        dt = _mybir.dt.from_np(_np.dtype(dtype))
        args.append(nc.dram_tensor(f"out_{i}_dram", shape, dt, kind="ExternalOutput").ap())
    layer_kernel(nc, *args)
    r = _run(nc, [arrays], core_ids=[0])
    got = tuple(r.results[0][f"out_{i}_dram"] for i in range(len(_OUTS)))
    return got[0]
```

```python
import concourse.bass as bass
from concourse import mybir
from contextlib import ExitStack

F32 = mybir.dt.float32
F32R = mybir.dt.float32r
ALU = mybir.AluOpType
ACT = mybir.ActivationFunctionType
AX = mybir.AxisListType


def begun(value):
    return not isinstance(value, int) or value > 0


def layer_kernel(nc, x, W_in, conv_w, conv_b, W_x, W_dt, b_dt, A_log, D, W_out,
                 gate_w, wg, wu, wd, swg, swu, swd, out):
    P = 128
    NB, L, DM = x.shape
    DI = conv_w.shape[0]
    NH = DI // P
    TAPS = conv_w.shape[2]
    NS = A_log.shape[1]
    DR = W_dt.shape[0]
    XP = DR + 2 * NS
    NE, _, FE = wg.shape
    FS = swg.shape[1]
    NQ = L // P
    GS = 4
    NG = NS // GS
    UNITS = NG * NH
    RING = 4
    BC = 2
    QE = P // NE
    SHARED = [min(P, FS - P * j) for j in range((FS + P - 1) // P)]
    NSH = len(SHARED)
    TILES = NSH + FE // QE
    ROUTED = TILES - NSH
    AR = 5
    EPS = 1e-5
    WARM = 30
    FILL = 9
    EXP_LOG, SILU = "natural_log_exp_and_others", "silu_and_others"
    assert DM == P and UNITS % RING == 0 and NG % BC == 0 and TILES % 2 == 0
    assert FE == ROUTED * QE and NH == 2 and NQ == 4

    with ExitStack() as ctx:
        def sb(name, shape, dtype=F32):
            return ctx.enter_context(nc.sbuf_tensor(name, shape, dtype))

        def psum(name, shape):
            return ctx.enter_context(nc.psum_tensor(name, shape, F32))

        def sem(name):
            return ctx.enter_context(nc.semaphore(name))

        w_taps = sb("w_taps", [P, TAPS, DI])
        w_z = sb("w_z", [P, DI])
        w_x = sb("w_x", [P, NH, XP])
        w_dt = sb("w_dt", [DR, DI])
        w_out = sb("w_out", [P, NH, DM])
        cb = sb("cb", [P, NH])
        bdt = sb("bdt", [P, NH])
        a_neg = sb("a_neg", [P, NH, NS])
        a_exp = sb("a_exp", [P, NH, NS])
        d_skip = sb("d_skip", [P, NH])
        gate = sb("gate", [P, NE])
        w_gate_hi, w_gate_lo, w_up_hi, w_up_lo = (
            sb(name, [P, P, ROUTED], F32R) for name in ("w_gate_hi", "w_gate_lo", "w_up_hi", "w_up_lo"))
        s_gate_hi, s_gate_lo, s_up_hi, s_up_lo = (
            sb(name, [P, FS], F32R) for name in ("s_gate_hi", "s_gate_lo", "s_up_hi", "s_up_lo"))
        w_down = sb("w_down", [P, ROUTED, DM])
        s_down = sb("s_down", [P, NSH, DM])
        ident = sb("ident", [P, P])
        lower = sb("lower", [P, NQ, NE, NE])
        neg_half = sb("neg_half", [P, NQ])
        waited = sb("waited", [P, 1])
        xln = sb("xln", [P, NQ, DM])
        xnT = sb("xnT", [P, TAPS - 1 + L])
        stA = sb("stA", [P, NQ, 6])
        mvA = sb("mvA", [P, NQ, 2])
        rsA = sb("rsA", [P, NQ])
        nmA = sb("nmA", [P, NQ])
        sp_1t = sb("sp_1t", [P, NH, L])
        xc = sb("xc", [P, NH, L])
        xcD = sb("xcD", [P, NH, L])
        sp_log = xcD
        xproj = sb("xproj", [XP, L])
        dt = sb("dt", [P, NH, L])
        u = sb("u", [P, NH, L])
        dA = sb("dA", [P, RING, GS, L])
        w_gate, w_up = (dA[:, n].rearrange("p s l -> p (s l)")[:, 0:P * ROUTED] for n in range(2))
        s_gate, s_up = (dA[:, 2 + n].rearrange("p s l -> p (s l)")[:, 0:FS] for n in range(2))
        hb = sb("hb", [P, RING, GS, L])
        w_xi = hb[:, 0, 0, 0:DI]
        cw_all = hb[:, 1].rearrange("p s l -> p (s l)")[:, 0:DI * TAPS]
        b_all = sb("b_all", [P, BC, GS, L])
        c_all = sb("c_all", [P, BC, GS, L])
        zg = sb("zg", [P, NQ, DI])
        yg = sb("yg", [P, NQ, DI])
        ygT = sb("ygT", [P, NH, L])
        sp_r = yg[:].rearrange("p q d -> p (q d)").rearrange("p (h l) -> p h l", h=NH)
        sp_t = ygT
        o_sb = sb("o_sb", [P, NQ, DM])
        stO = sb("stO", [P, NQ, 6])
        mvO = sb("mvO", [P, NQ, 2])
        rsO = sb("rsO", [P, NQ])
        nmO = sb("nmO", [P, NQ])
        st2 = sb("st2", [P, NQ, 6])
        mv2 = sb("mv2", [P, NQ, 2])
        rs2 = sb("rs2", [P, NQ])
        nm2 = sb("nm2", [P, NQ])
        x1 = sb("x1", [P, NQ, DM])
        x1T_hi = sb("x1T_hi", [P, L], F32R)
        x1T_lo = sb("x1T_lo", [P, L], F32R)
        x1n = o_sb
        o_flat = o_sb[:].rearrange("p q m -> p (q m)")
        x1T = o_flat
        r_max = sb("r_max", [P, NQ])
        r_sh = sb("r_sh", [P, NQ, NE])
        r_ex = sb("r_ex", [P, NQ, NE])
        r_sum = sb("r_sum", [P, NQ])
        r_inv = sb("r_inv", [P, NQ])
        r_sc = sb("r_sc", [P, NQ, NE])
        PAIRS = NQ * NE * NE
        r_gt, r_eq = (o_flat[:, PAIRS * n:PAIRS * n + PAIRS].rearrange("p (q e f) -> p q e f", e=NE, f=NE) for n in range(2))
        r_rank = sb("r_rank", [P, NQ, NE])
        r_top = sb("r_top", [P, NQ, NE])
        r_den = sb("r_den", [P, NQ])
        r_rden = sb("r_rden", [P, NQ])
        w_tok = o_sb
        w_feat = sb("w_feat", [P, L])
        silu_g = sb("silu_g", [P, 2, L])
        act = sb("act", [P, AR, L])
        x1_old = sb("x1_old", [P, NQ, DM])
        stG = sb("stG", [P, NQ, 6])
        mvG = sb("mvG", [P, NQ, 2])
        rsG = sb("rsG", [P, NQ])
        nmG = sb("nmG", [P, NQ])
        y_out = sb("y_out", [P, NQ, DM])

        bc_dram = nc.dram_tensor("bc_dram", (NB, 2 * NS, L), F32, kind="Internal").ap()

        y_ps = psum("y_ps", [P, NQ, DI])
        misc_bank = psum("misc_bank", [P, L])
        g_ps = psum("g_ps", [P, 2, L])
        u_ps = psum("u_ps", [P, 2, L])
        f_ps = psum("f_ps", [P, NQ, DM])

        taps_loaded, early_loaded, late_loaded = sem("taps_loaded"), sem("early_loaded"), sem("late_loaded")
        xln_loaded, xres_loaded = sem("xln_loaded"), sem("xres_loaded")
        bc_stored, x1_moved, y_stored = sem("bc_stored"), sem("x1_moved"), sem("y_stored")
        b_loaded = [sem(f"b_loaded{g}") for g in range(BC)]
        c_loaded = [sem(f"c_loaded{g}") for g in range(BC)]
        const_step, const_ready, a_ready_exp, a_ready = sem("const_step"), sem("const_ready"), sem("a_ready_exp"), sem("a_ready")
        zeros_ready, waited_step = sem("zeros_ready"), sem("waited_step")
        lnA_step, varA_ready, rsA_ready, xn_ready = sem("lnA_step"), sem("varA_ready"), sem("rsA_ready"), sem("xn_ready")
        xnT_ps, xnT_ready = sem("xnT_ps"), sem("xnT_ready")
        xi_ps = sem("xi_ps")
        xc_ready, xcD_ready = sem("xc_ready"), sem("xcD_ready")
        xp_ps, xp_ready = sem("xp_ps"), sem("xp_ready")
        dt_ps, dt_taken, sp_step, sp_ready = sem("dt_ps"), sem("dt_taken"), sem("sp_step"), sem("sp_ready")
        w_taps_ready, hi_ready, w_split, x1T_split = (
            sem("w_taps_ready"), sem("hi_ready"), sem("w_split"), sem("x1T_split"))
        sp_added, y_started, rmax_step = sem("sp_added"), sem("y_started"), sem("rmax_step")
        powA_done, powO_done, pow2_done, powG_done = sem("powA_done"), sem("powO_done"), sem("pow2_done"), sem("powG_done")
        dt_step, dt_ready, u_ready = sem("dt_step"), sem("dt_ready"), sem("u_ready")
        z_ps, z_ready = sem("z_ps"), sem("z_ready")
        dA_ready, bu_ready, scan_done, hc_ready, sum_done = (
            sem("dA_ready"), sem("bu_ready"), sem("scan_done"), sem("hc_ready"), sem("sum_done"))
        yg_ready, yT_ps, yT_ready, o_ps, o_ready = (
            sem("yg_ready"), sem("yT_ps"), sem("yT_ready"), sem("o_ps"), sem("o_ready"))
        lnO_step, varO_ready, rsO_ready, on_ready = sem("lnO_step"), sem("varO_ready"), sem("rsO_ready"), sem("on_ready")
        x1_ready = sem("x1_ready")
        ln2_step, var2_ready, rs2_ready, x1n_ready = sem("ln2_step"), sem("var2_ready"), sem("rs2_ready"), sem("x1n_ready")
        x1T_ps, x1T_ready, lg_ps, lg_taken = sem("x1T_ps"), sem("x1T_ready"), sem("lg_ps"), sem("lg_taken")
        rt_step, rex_ready, w_ready, wf_ps, wf_ready = (
            sem("rt_step"), sem("rex_ready"), sem("w_ready"), sem("wf_ps"), sem("wf_ready"))
        gate_ps, up_ps, silu_ready, act_ready, actw_ready, down_done = (
            sem("gate_ps"), sem("up_ps"), sem("silu_ready"), sem("act_ready"), sem("actw_ready"), sem("down_done"))
        lnG_step, varG_ready, rsG_ready, f_taken, y_ready = (
            sem("lnG_step"), sem("varG_ready"), sem("rsG_ready"), sem("f_taken"), sem("y_ready"))

        tokens = lambda ap: ap.rearrange("(q p) m -> p q m", p=P)
        flat = lambda t: t[:] if len(t.shape) == 2 else t[:].rearrange("p f j -> p (f j)")
        halves = lambda ap: ap.rearrange("(h p) n -> p h n", p=P)

        LN_STEPS = 2 * NQ
        RT_STEPS = 12
        EARLY, LATE = 9, 5 + NSH

        def live(b):
            return not isinstance(b, int) or 0 <= b < NB

        def run(engine, iteration):
            for i in range(-1, 3):
                iteration(i)
            with engine.Fori(3, NB - 1) as i:
                iteration(i)
            for i in range(NB - 1, NB + 2):
                iteration(i)

        block = ctx.enter_context(nc.Block())

        @block.sync
        def _(sp):
            def load_x(b, first=False):
                if not live(b) or (isinstance(b, int) and b == 0 and not first):
                    return
                if begun(b):
                    sp.wait_ge(xnT_ps, b)
                sp.dma_start(xln[:], tokens(x[b])).then_inc(xln_loaded, 16)

            load_x(0, first=True)
            with nc.allow_non_contiguous_dma(reason="a few small vectors, once"):
                for to, of in ((w_xi, W_in[:, 0:DI]),
                               (cw_all, conv_w.rearrange("d o k -> (d o k)").unsqueeze(0).broadcast_to([P, DI * TAPS]))):
                    sp.dma_start(to, of).then_inc(taps_loaded, 16)
                for to, of in ((cb[:], conv_b.rearrange("(h p) -> p h", p=P)),
                               (w_x[:], halves(W_x)), (w_dt[:], W_dt),
                               (bdt[:], b_dt.rearrange("(h p) -> p h", p=P)),
                               (a_exp[:], halves(A_log)),
                               (w_z[:], W_in[:, DI:2 * DI]),
                               (d_skip[:], D.rearrange("(h p) -> p h", p=P)),
                               (w_out[:], halves(W_out)),
                               (gate[:], gate_w.rearrange("e m -> m e"))):
                    sp.dma_start(to, of).then_inc(early_loaded, 16)
            sp.dma_start(w_gate.rearrange("p (e r) -> p e r", e=NE),
                         wg.rearrange("e m r -> m e r")).then_inc(late_loaded, 16)
            sp.dma_start(w_up.rearrange("p (e r) -> p e r", e=NE),
                         wu.rearrange("e m r -> m e r")).then_inc(late_loaded, 16)
            sp.dma_start(s_gate, swg).then_inc(late_loaded, 16)
            sp.dma_start(s_up, swu).then_inc(late_loaded, 16)
            for j, n in enumerate(SHARED):
                sp.dma_start(s_down[0:n, j, :], swd[P * j:P * j + n, :]).then_inc(late_loaded, 16)
            sp.dma_start(w_down[:], wd.rearrange("e r h -> (e r) h").rearrange("(p j) h -> p j h", p=P))\
              .then_inc(late_loaded, 16)

            def store_bc(b):
                if not live(b):
                    return
                sp.wait_ge(xp_ready, b + 1)
                sp.dma_start(bc_dram[b], xproj[DR:XP, :]).then_inc(bc_stored, 16)

            def load_b(b, g):
                if not live(b):
                    return
                if g == 0:
                    sp.wait_ge(bc_stored, 16 * (b + 1))
                if begun(NH * (NG * b + g - BC + 1)):
                    sp.wait_ge(bu_ready, NH * (NG * b + g - BC + 1))
                sp.dma_start(b_all[:, g % BC].rearrange("p s l -> p (s l)"),
                             bc_dram[b, GS * g:GS * g + GS, :].rearrange("s l -> (s l)").unsqueeze(0)
                             .broadcast_to([P, GS * L])).then_inc(b_loaded[g % BC], 16)

            def load_c(b, g):
                if not live(b):
                    return
                if g == 0:
                    sp.wait_ge(bc_stored, 16 * (b + 1))
                if begun(NH * (NG * b + g - BC + 1)):
                    sp.wait_ge(hc_ready, NH * (NG * b + g - BC + 1))
                sp.dma_start(c_all[:, g % BC].rearrange("p s l -> p (s l)"),
                             bc_dram[b, NS + GS * g:NS + GS * g + GS, :].rearrange("s l -> (s l)").unsqueeze(0)
                             .broadcast_to([P, GS * L])).then_inc(c_loaded[g % BC], 16)

            def load_xres(b):
                if not live(b):
                    return
                if begun(16 * b):
                    sp.wait_ge(x1_moved, 16 * b)
                if begun(b):
                    sp.wait_ge(x1n_ready, b)
                sp.dma_start(x1[:], tokens(x[b])).then_inc(xres_loaded, 16)

            def move_x1(b):
                if not live(b):
                    return
                sp.wait_ge(x1_ready, b + 1)
                sp.dma_start(x1_old[:], x1[:]).then_inc(x1_moved, 16)

            def store_y(b):
                if not live(b):
                    return
                sp.wait_ge(y_ready, b + 1)
                sp.dma_start(tokens(out[b]), y_out[:]).then_inc(y_stored, 16)

            def iteration(i):
                nxt, cur, old, older = i + 1, i, i - 1, i - 2
                load_x(nxt)
                load_c(cur, 0)
                move_x1(older)
                load_b(cur, 1)
                load_c(cur, 1)
                load_b(cur, 2)
                load_c(cur, 2)
                load_xres(old)
                load_b(cur, 3)
                load_c(cur, 3)
                store_bc(nxt)
                load_b(nxt, 0)
                store_y(older)

            run(sp, iteration)
            sp.wait_ge(y_stored, 16 * NB)

        @block.gpsimd
        def _(pool):
            nc.gpsimd.memset(neg_half[:], -0.5).then_inc(const_step, 1)
            nc.gpsimd.memset(ident[:], 0.0).then_inc(const_step, 1)
            nc.gpsimd.memset(lower[:], 1.0).then_inc(const_step, 1)
            pool.wait_ge(const_step, 3)
            nc.gpsimd.affine_select(out=ident[:], in_=ident[:], compare_op=ALU.not_equal, fill=1.0, base=0,
                                    pattern=[[-1, P]], channel_multiplier=1).then_inc(const_ready, 1)
            nc.gpsimd.affine_select(out=lower[:], in_=lower[:], compare_op=ALU.is_gt, fill=0.0, base=0,
                                    pattern=[[0, NQ], [1, NE], [-1, NE]], channel_multiplier=0).then_inc(const_ready, 1)

            def scales(b, rs, nm, var_ready, pow_done, rs_ready):
                if not live(b):
                    return
                pool.wait_ge(var_ready, b + 1)
                nc.gpsimd.tensor_tensor(rs[:], rs[:], neg_half[:], ALU.pow).then_inc(pow_done, 1)
                pool.wait_ge(pow_done, b + 1)
                nc.gpsimd.tensor_tensor(nm[:], nm[:], rs[:], ALU.mult).then_inc(rs_ready, 1)

            def scales_x(b):
                scales(b, rsA, nmA, varA_ready, powA_done, rsA_ready)

            def scales_o(b):
                scales(b, rsO, nmO, varO_ready, powO_done, rsO_ready)

            def scales_x1(b):
                scales(b, rs2, nm2, var2_ready, pow2_done, rs2_ready)

            def scales_f(b):
                scales(b, rsG, nmG, varG_ready, powG_done, rsG_ready)

            def add_relu(b):
                if not live(b):
                    return
                pool.wait_ge(sp_ready, b + 1)
                nc.gpsimd.tensor_tensor(sp_log[:], sp_log[:], sp_r[:], ALU.add).then_inc(sp_added, 1)

            def make_u(b):
                if not live(b):
                    return
                pool.wait_ge(dt_ready, b + 1)
                pool.wait_ge(xc_ready, NH * (b + 1))
                if begun(UNITS * b):
                    pool.wait_ge(bu_ready, UNITS * b)
                nc.gpsimd.tensor_tensor(u[:], dt[:], xc[:], ALU.mult).then_inc(u_ready, 1)

            def bu(b, k):
                if not live(b):
                    return
                g, h = k // NH, k % NH
                if k == 0:
                    pool.wait_ge(u_ready, b + 1)
                if h == 0:
                    pool.wait_ge(b_loaded[g % BC], 16 * (NG // BC * b + g // BC + 1))
                if begun(UNITS * b + k + 1 - RING):
                    pool.wait_ge(sum_done, UNITS * b + k + 1 - RING)
                nc.gpsimd.tensor_tensor(hb[:, k % RING], u[:, h, :].unsqueeze(1).broadcast_to([P, GS, L]),
                                        b_all[:, g % BC], ALU.mult).then_inc(bu_ready, 1)

            def weigh(b, j):
                if not live(b):
                    return
                pool.wait_ge(act_ready, TILES * b + j + 1)
                if j == NSH:
                    pool.wait_ge(wf_ready, b + 1)
                nc.gpsimd.tensor_tensor(act[:, j % AR], act[:, j % AR], w_feat[:], ALU.mult).then_inc(actw_ready, 1)

            def iteration(i):
                nxt, cur, old, older = i + 1, i, i - 1, i - 2
                scales_x(nxt)
                bu(cur, 1)
                weigh(older, 5)
                bu(cur, 2)
                bu(cur, 3)
                scales_o(old)
                weigh(older, 6)
                bu(cur, 4)
                weigh(older, 7)
                bu(cur, 5)
                scales_x1(old)
                bu(cur, 6)
                weigh(older, 8)
                weigh(older, 9)
                weigh(older, 10)
                weigh(older, 11)
                weigh(older, 12)
                weigh(older, 13)
                bu(cur, 7)
                add_relu(nxt)
                scales_f(older)
                make_u(nxt)
                bu(nxt, 0)
                weigh(old, 3)
                weigh(old, 4)

            run(pool, iteration)

        @block.scalar
        def _(acte):
            A = nc.scalar

            loaded = None

            def table(name, *batches):
                nonlocal loaded
                if name != loaded and any(live(b) for b in batches):
                    A.preload_act_table_set(name)
                    loaded = name

            def normalize(dst, src, rs, nm, done):
                for q in range(NQ):
                    last = A.activation(dst[:, q], src[:, q], ACT.Identity, scale=rs[:, q:q + 1], bias=nm[:, q:q + 1])
                last.then_inc(done, 1)

            def normalize_x(b, first=False):
                if not live(b) or (isinstance(b, int) and b == 0 and not first):
                    return
                acte.wait_ge(rsA_ready, b + 1)
                normalize(xln, xln, rsA, nmA, xn_ready)

            def take_xnT(b):
                if not live(b):
                    return
                acte.wait_ge(xnT_ps, b + 1)
                if begun(NH * b):
                    acte.wait_ge(xi_ps, NH * b)
                if begun(2 * b):
                    acte.wait_ge(z_ps, 2 * b)
                A.copy(xnT[:, TAPS - 1:], misc_bank[:]).then_inc(xnT_ready, 1)

            def silu_conv(b, h):
                if not live(b):
                    return
                acte.wait_ge(xi_ps, NH * b + h + 1)
                if begun(b):
                    acte.wait_ge(u_ready, b)
                if begun(b):
                    acte.wait_ge(xcD_ready, b)
                A.activation(xc[:, h], misc_bank[:], ACT.Silu, bias=cb[:, h:h + 1]).then_inc(xc_ready, 1)

            def skip(b):
                if not live(b):
                    return
                acte.wait_ge(xc_ready, NH * (b + 1))
                acte.wait_ge(dt_ready, b + 1)
                for h in range(NH):
                    last = A.activation(xcD[:, h], xc[:, h], ACT.Copy, scale=d_skip[:, h:h + 1])
                last.then_inc(xcD_ready, 1)

            def take_xproj(b):
                if not live(b):
                    return
                acte.wait_ge(xp_ps, b + 1)
                if begun(NH * b):
                    acte.wait_ge(dt_ps, NH * b)
                if begun(16 * b):
                    acte.wait_ge(bc_stored, 16 * b)
                A.copy(xproj[:], misc_bank[0:XP, :]).then_inc(xp_ready, 1)

            def take_dt(b, h):
                if not live(b):
                    return
                acte.wait_ge(dt_ps, NH * b + h + 1)
                if begun(b - 1):
                    acte.wait_ge(o_ps, b - 1)
                A.activation(sp_t[:, h], misc_bank[:], ACT.Abs, bias=bdt[:, h:h + 1])
                A.activation(sp_r[:, h], misc_bank[:], ACT.Relu, bias=bdt[:, h:h + 1]).then_inc(dt_taken, 1)

            def softplus_log(b):
                if not live(b):
                    return
                acte.wait_ge(dt_taken, NH * (b + 1))
                if isinstance(b, int) and b == 0:
                    A.activation(a_neg[:], a_exp[:], ACT.Exp).then_inc(a_ready_exp, 1)
                if begun(b):
                    acte.wait_ge(dt_ready, b)
                if begun(b):
                    acte.wait_ge(y_started, b)
                A.activation(sp_t[:], sp_t[:], ACT.Exp, scale=-1.0).then_inc(sp_step, 1)
                acte.wait_ge(sp_step, 2 * b + 1)
                A.activation(sp_1t[:], sp_t[:], ACT.Identity, bias=1.0).then_inc(sp_step, 1)
                acte.wait_ge(sp_step, 2 * b + 2)
                A.activation(sp_log[:], sp_1t[:], ACT.Ln).then_inc(sp_ready, 1)

            def discount(b, k):
                if not live(b):
                    return
                g, h = k // NH, k % NH
                if begun(UNITS * b + k + 1 - RING):
                    acte.wait_ge(scan_done, UNITS * b + k + 1 - RING)
                if k == 0:
                    acte.wait_ge(dt_ready, b + 1)
                for s in range(GS):
                    last = A.activation(dA[:, k % RING, s, 1:L], dt[:, h, 1:L], ACT.Exp,
                                        scale=a_neg[:, h, GS * g + s:GS * g + s + 1])
                last.then_inc(dA_ready, 1)

            def silu_z(b, m):
                if not live(b):
                    return
                acte.wait_ge(z_ps, 2 * b + m + 1)
                if begun(b):
                    acte.wait_ge(yg_ready, b)
                A.activation(zg[:, 2 * m:2 * m + 2].rearrange("p q d -> p (q d)"), misc_bank[:],
                             ACT.Silu).then_inc(z_ready, 1)

            def take_yT(b, h):
                if not live(b):
                    return
                acte.wait_ge(yT_ps, NH * b + h + 1)
                if begun(b):
                    acte.wait_ge(o_ps, b)
                A.copy(ygT[:, h], misc_bank[:]).then_inc(yT_ready, 1)

            def take_o(b):
                if not live(b):
                    return
                acte.wait_ge(o_ps, b + 1)
                if begun(b):
                    acte.wait_ge(wf_ps, b)
                A.copy(o_sb[:].rearrange("p q m -> p (q m)"), misc_bank[:]).then_inc(o_ready, 1)

            def normalize_o(b):
                if not live(b):
                    return
                acte.wait_ge(rsO_ready, b + 1)
                normalize(o_sb, o_sb, rsO, nmO, on_ready)

            def normalize_x1(b):
                if not live(b):
                    return
                acte.wait_ge(rs2_ready, b + 1)
                normalize(x1n, x1, rs2, nm2, x1n_ready)

            def take_x1T(b):
                if not live(b):
                    return
                acte.wait_ge(x1T_ps, b + 1)
                if begun(TILES * b):
                    acte.wait_ge(gate_ps, TILES * b)
                if begun(TILES * b):
                    acte.wait_ge(up_ps, TILES * b)
                A.copy(x1T_hi[:], misc_bank[:])
                A.copy(x1T, misc_bank[:]).then_inc(x1T_ready, 1)

            def router_exp(b):
                if not live(b):
                    return
                acte.wait_ge(lg_taken, b + 1)
                if begun(b):
                    acte.wait_ge(w_ready, b)
                A.activation(r_ex[:], r_sh[:], ACT.Exp).then_inc(rex_ready, 1)

            def take_w_feat(b):
                if not live(b):
                    return
                acte.wait_ge(wf_ps, b + 1)
                if begun(ROUTED * b):
                    acte.wait_ge(actw_ready, ROUTED * b)
                A.copy(w_feat[:], misc_bank[:]).then_inc(wf_ready, 1)

            def silu_tile(b, j):
                if not live(b):
                    return
                n = TILES * b + j
                rows = SHARED[j] if j < NSH else P
                acte.wait_ge(gate_ps, n + 1)
                if begun(n - 1):
                    acte.wait_ge(act_ready, n - 1)
                A.activation(silu_g[0:rows, j % 2], g_ps[0:rows, j % 2], ACT.Silu).then_inc(silu_ready, 1)

            def normalize_f(b):
                if not live(b):
                    return
                acte.wait_ge(rsG_ready, b + 1)
                if begun(16 * b):
                    acte.wait_ge(y_stored, 16 * b)
                normalize(y_out, f_ps, rsG, nmG, f_taken)

            def iteration(i):
                nxt, cur, old, older = i + 1, i, i - 1, i - 2
                discount(cur, 1)
                take_yT(old, 0)
                table(SILU, older, cur)
                silu_tile(older, 5)
                take_yT(old, 1)
                silu_tile(older, 6)
                silu_z(cur, 0)
                skip(cur)
                silu_z(cur, 1)
                silu_tile(older, 7)
                normalize_x(nxt)
                silu_tile(older, 8)
                take_o(old)
                table(EXP_LOG, cur)
                discount(cur, 2)
                take_xnT(nxt)
                discount(cur, 3)
                discount(cur, 4)
                table(SILU, older, nxt)
                silu_tile(older, 9)
                silu_conv(nxt, 0)
                normalize_o(old)
                table(EXP_LOG, cur)
                discount(cur, 5)
                table(SILU, older, nxt)
                silu_tile(older, 10)
                silu_tile(older, 11)
                silu_conv(nxt, 1)
                table(EXP_LOG, cur)
                discount(cur, 6)
                normalize_x1(old)
                take_xproj(nxt)
                table(SILU, older)
                silu_tile(older, 12)
                take_x1T(old)
                silu_tile(older, 13)
                table(EXP_LOG, cur, old, nxt)
                discount(cur, 7)
                router_exp(old)
                take_dt(nxt, 0)
                take_dt(nxt, 1)
                softplus_log(nxt)
                table(SILU, old)
                silu_tile(old, 0)
                silu_tile(old, 1)
                silu_tile(old, 2)
                normalize_f(older)
                take_w_feat(old)
                silu_tile(old, 3)
                silu_tile(old, 4)
                table(EXP_LOG, nxt)
                discount(nxt, 0)

            table(SILU, 0)
            normalize_x(0, first=True)
            acte.wait_ge(early_loaded, 16 * EARLY)
            run(acte, iteration)

        @block.vector
        def _(dve):
            V = nc.vector
            V.memset(xnT[:, 0:TAPS - 1], 0.0).then_inc(zeros_ready, 1)

            def stats(b, src, st, mv, rs, nm, step, ready):
                for q in range(NQ):
                    V.bn_stats(st[:, q], src[:, q]).then_inc(step, 1)
                dve.wait_ge(step, LN_STEPS * b + NQ)
                V.memset(waited[:], 0.0).then_inc(waited_step, 1)
                for q in range(NQ):
                    V.bn_aggr(mv[:, q], st[:, q]).then_inc(step, 1)
                dve.wait_ge(step, LN_STEPS * b + 2 * NQ)
                V.tensor_scalar(nm[:], mv[:, :, 0], -1.0, None, ALU.mult)
                V.tensor_scalar(rs[:], mv[:, :, 1], EPS, None, ALU.add).then_inc(ready, 1)

            def stats_x(b, first=False):
                if not live(b) or (isinstance(b, int) and b == 0 and not first):
                    return
                dve.wait_ge(xln_loaded, 16 * (b + 1))
                if begun(b):
                    dve.wait_ge(xn_ready, b)
                stats(b, xln, stA, mvA, rsA, nmA, lnA_step, varA_ready)

            def stats_o(b):
                if not live(b):
                    return
                dve.wait_ge(o_ready, b + 1)
                stats(b, o_sb, stO, mvO, rsO, nmO, lnO_step, varO_ready)

            def stats_x1(b):
                if not live(b):
                    return
                dve.wait_ge(x1_ready, b + 1)
                stats(b, x1, st2, mv2, rs2, nm2, ln2_step, var2_ready)

            def stats_f(b):
                if not live(b):
                    return
                dve.wait_ge(down_done, TILES * (b + 1))
                stats(b, f_ps, stG, mvG, rsG, nmG, lnG_step, varG_ready)

            def split_tokens(b):
                if not live(b):
                    return
                dve.wait_ge(x1T_ready, b + 1)
                V.tensor_tensor(x1T_lo[:], x1T, x1T_hi[:].bitcast(F32), ALU.subtract).then_inc(x1T_split, 1)

            def split_weights():
                dve.wait_ge(late_loaded, 16 * LATE)
                for full, hi, lo in ((s_gate, s_gate_hi, s_gate_lo), (s_up, s_up_hi, s_up_lo),
                                     (w_gate, w_gate_hi, w_gate_lo), (w_up, w_up_hi, w_up_lo)):
                    V.tensor_copy(flat(hi), full).then_inc(hi_ready, 1)
                dve.wait_ge(hi_ready, 4)
                for full, hi, lo in ((s_gate, s_gate_hi, s_gate_lo), (s_up, s_up_hi, s_up_lo),
                                     (w_gate, w_gate_hi, w_gate_lo), (w_up, w_up_hi, w_up_lo)):
                    V.tensor_tensor(flat(lo), full, flat(hi).bitcast(F32), ALU.subtract).then_inc(w_split, 1)
                dve.wait_ge(w_split, 4)
                V.memset(dA[:, :, :, 0:1], 0.0).then_inc(zeros_ready, 1)

            def make_dt(b):
                if not live(b):
                    return
                if isinstance(b, int) and b == 0:
                    split_weights()
                dve.wait_ge(sp_ready, b + 1)
                V.scalar_tensor_tensor(sp_1t[:], sp_1t[:], -1.0, sp_t[:], ALU.add, ALU.subtract).then_inc(dt_step, 1)
                if isinstance(b, int) and b == 0:
                    dve.wait_ge(a_ready_exp, 1)
                    V.tensor_scalar(a_neg[:], a_neg[:], -1.0, None, ALU.mult).then_inc(a_ready, 1)
                dve.wait_ge(dt_step, b + 1)
                dve.wait_ge(sp_added, b + 1)
                if begun(UNITS * b):
                    dve.wait_ge(dA_ready, UNITS * b)
                if begun(b):
                    dve.wait_ge(u_ready, b)
                V.tensor_tensor(dt[:], sp_log[:], sp_1t[:], ALU.subtract).then_inc(dt_ready, 1)

            def scan(b, k):
                if not live(b):
                    return
                dve.wait_ge(dA_ready, UNITS * b + k + 1)
                dve.wait_ge(bu_ready, UNITS * b + k + 1)
                h_of = hb[:, k % RING].rearrange("p s l -> p (s l)")
                V.tensor_tensor_scan(h_of, dA[:, k % RING].rearrange("p s l -> p (s l)"), h_of, 0.0,
                                     ALU.mult, ALU.add).then_inc(scan_done, 1)

            def times_c(b, k):
                if not live(b):
                    return
                g = k // NH
                if k % NH == 0:
                    dve.wait_ge(c_loaded[g % BC], 16 * (NG // BC * b + g // BC + 1))
                dve.wait_ge(scan_done, UNITS * b + k + 1)
                V.tensor_tensor(hb[:, k % RING], hb[:, k % RING], c_all[:, g % BC], ALU.mult).then_inc(hc_ready, 1)

            def gate_y(b):
                if not live(b):
                    return
                dve.wait_ge(sum_done, UNITS * (b + 1))
                dve.wait_ge(z_ready, 2 * (b + 1))
                if begun(NH * b):
                    dve.wait_ge(yT_ps, NH * b)
                dve.wait_ge(dt_ready, min(b + 2, NB) if isinstance(b, int) else b + 2)
                V.tensor_tensor(yg[:], y_ps[:], zg[:], ALU.mult).then_inc(yg_ready, 1)

            def add_x(b):
                if not live(b):
                    return
                dve.wait_ge(on_ready, b + 1)
                dve.wait_ge(xres_loaded, 16 * (b + 1))
                V.tensor_tensor(x1[:], o_sb[:], x1[:], ALU.add).then_inc(x1_ready, 1)

            def router_max(b):
                if not live(b):
                    return
                over = lambda ap: ap.unsqueeze(2).broadcast_to([P, NQ, NE])
                dve.wait_ge(lg_ps, b + 1)
                logits = misc_bank[:, 0:NQ * NE].rearrange("p (q e) -> p q e", e=NE)
                V.tensor_reduce(r_max[:], logits, AX.X, ALU.max).then_inc(rmax_step, 1)
                dve.wait_ge(rmax_step, b + 1)
                V.tensor_tensor(r_sh[:], logits, over(r_max[:]), ALU.subtract).then_inc(lg_taken, 1)

            def router_weights(b):
                if not live(b):
                    return
                count = 0

                def step(instruction):
                    nonlocal count
                    count += 1
                    instruction.then_inc(rt_step, 1)

                over = lambda ap: ap.unsqueeze(2).broadcast_to([P, NQ, NE])
                dve.wait_ge(rex_ready, b + 1)
                dve.wait_ge(x1T_split, b + 1)
                step(V.tensor_reduce(r_sum[:], r_ex[:], AX.X, ALU.add))
                dve.wait_ge(rt_step, RT_STEPS * b + count)
                step(V.reciprocal(r_inv[:], r_sum[:]))
                dve.wait_ge(rt_step, RT_STEPS * b + count)
                step(V.tensor_tensor(r_sc[:], r_ex[:], over(r_inv[:]), ALU.mult))
                other = r_sc[:].unsqueeze(2).broadcast_to([P, NQ, NE, NE])
                own = r_sc[:].unsqueeze(3).broadcast_to([P, NQ, NE, NE])
                dve.wait_ge(rt_step, RT_STEPS * b + count)
                step(V.tensor_tensor(r_gt, other, own, ALU.is_gt))
                step(V.tensor_tensor(r_eq, other, own, ALU.is_equal))
                dve.wait_ge(rt_step, RT_STEPS * b + count)
                step(V.tensor_tensor(r_eq, r_eq, lower[:], ALU.mult))
                dve.wait_ge(rt_step, RT_STEPS * b + count)
                step(V.tensor_tensor(r_gt, r_gt, r_eq, ALU.add))
                dve.wait_ge(rt_step, RT_STEPS * b + count)
                step(V.tensor_reduce(r_rank[:], r_gt, AX.X, ALU.add))
                dve.wait_ge(rt_step, RT_STEPS * b + count)
                step(V.scalar_tensor_tensor(r_top[:], r_rank[:], 2.0, r_sc[:], ALU.is_lt, ALU.mult))
                dve.wait_ge(rt_step, RT_STEPS * b + count)
                step(V.tensor_reduce(r_den[:], r_top[:], AX.X, ALU.add))
                dve.wait_ge(rt_step, RT_STEPS * b + count)
                step(V.tensor_scalar(r_den[:], r_den[:], 1e-20, None, ALU.add))
                dve.wait_ge(rt_step, RT_STEPS * b + count)
                step(V.reciprocal(r_rden[:], r_den[:]))
                assert count == RT_STEPS
                dve.wait_ge(rt_step, RT_STEPS * b + count)
                V.tensor_tensor(w_tok[:].rearrange("p q (e r) -> p q e r", e=NE),
                                r_top[:].unsqueeze(3).broadcast_to([P, NQ, NE, QE]),
                                r_rden[:].unsqueeze(2).unsqueeze(3).broadcast_to([P, NQ, NE, QE]),
                                ALU.mult).then_inc(w_ready, 1)

            def times_up(b, j):
                if not live(b):
                    return
                n = TILES * b + j
                rows = SHARED[j] if j < NSH else P
                dve.wait_ge(silu_ready, n + 1)
                dve.wait_ge(up_ps, n + 1)
                last = j - AR if j >= AR else j + (TILES - 1 - j) // AR * AR - TILES
                if begun(TILES * b + last + 1):
                    dve.wait_ge(down_done, TILES * b + last + 1)
                V.tensor_tensor(act[0:rows, j % AR], silu_g[0:rows, j % 2], u_ps[0:rows, j % 2],
                                ALU.mult).then_inc(act_ready, 1)

            def add_x1(b):
                if not live(b):
                    return
                dve.wait_ge(f_taken, b + 1)
                dve.wait_ge(x1_moved, 16 * (b + 1))
                V.tensor_tensor(y_out[:], y_out[:], x1_old[:], ALU.add).then_inc(y_ready, 1)

            stats_x(0, first=True)
            dve.wait_ge(taps_loaded, 16 * 2)
            V.tensor_tensor(w_taps[:], w_xi.unsqueeze(1).broadcast_to([P, TAPS, DI]),
                            cw_all.rearrange("p (d k) -> p k d", k=TAPS), ALU.mult).then_inc(w_taps_ready, 1)
            dve.wait_ge(const_ready, 2)

            def iteration(i):
                nxt, cur, old, older = i + 1, i, i - 1, i - 2
                times_up(older, 4)
                stats_x(nxt)
                scan(cur, 0)
                times_up(older, 5)
                times_c(cur, 0)
                times_up(older, 6)
                scan(cur, 1)
                times_c(cur, 1)
                times_up(older, 7)
                stats_o(old)
                times_up(older, 8)
                scan(cur, 2)
                times_c(cur, 2)
                scan(cur, 3)
                times_c(cur, 3)
                times_up(older, 9)
                add_x(old)
                scan(cur, 4)
                stats_x1(old)
                times_c(cur, 4)
                times_up(older, 10)
                scan(cur, 5)
                times_up(older, 11)
                times_c(cur, 5)
                scan(cur, 6)
                times_up(older, 12)
                router_max(old)
                times_up(older, 13)
                split_tokens(old)
                times_c(cur, 6)
                router_weights(old)
                stats_f(older)
                scan(cur, 7)
                times_up(old, 0)
                make_dt(nxt)
                times_up(old, 1)
                times_up(old, 2)
                add_x1(older)
                times_c(cur, 7)
                times_up(old, 3)
                gate_y(cur)

            run(dve, iteration)

        @block.tensor
        def _(pe):
            T = nc.tensor

            misc = {
                "wf": (-2, wf_ready, 1, 1),
                "yT0": (-1, yT_ready, NH, 1),
                "yT1": (-1, yT_ready, NH, 2),
                "z0": (0, z_ready, 2, 1),
                "z1": (0, z_ready, 2, 2),
                "o": (-1, o_ready, 1, 1),
                "xnT": (1, xnT_ready, 1, 1),
                "xi0": (1, xc_ready, NH, 1),
                "xi1": (1, xc_ready, NH, 2),
                "xp": (1, xp_ready, 1, 1),
                "x1T": (-1, x1T_ready, 1, 1),
                "lg": (-1, lg_taken, 1, 1),
                "dt0": (1, dt_taken, NH, 1),
                "dt1": (1, dt_taken, NH, 2),
            }
            uses = list(misc)

            def misc_free(name, b):
                i, at = b - misc[name][0], uses.index(name)
                order = [(n, i - 1 + misc[n][0]) for n in uses] + [(n, i + misc[n][0]) for n in uses[:at]]
                order = [(n, before) for n, before in order if live(before)]
                if order:
                    n, before = order[-1]
                    _, taken, per_batch, count = misc[n]
                    pe.wait_ge(taken, per_batch * before + count)

            def transposed(src, dst, done):
                for q in range(NQ):
                    last = T.transpose(dst[:, P * q:P * q + P], src(q), ident[:])
                last.then_inc(done, 1)

            def transpose_xn(b, first=False):
                if not live(b) or (isinstance(b, int) and b == 0 and not first):
                    return
                pe.wait_ge(xn_ready, b + 1)
                misc_free("xnT", b)
                transposed(lambda q: xln[:, q], misc_bank, xnT_ps)

            def busy(n):
                for m in range(n):
                    T.transpose(f_ps[:, m % NQ], ident[:], ident[:])

            def project_xi(b, h):
                if not live(b):
                    return
                pe.wait_ge(xnT_ready, b + 1)
                misc_free(f"xi{h}", b)
                for tap in range(TAPS):
                    last = T.matmul(misc_bank[:], w_taps[:, tap, P * h:P * h + P], xnT[:, tap:tap + L],
                                    start=(tap == 0), stop=(tap == TAPS - 1))
                last.then_inc(xi_ps, 1)

            def project_x(b):
                if not live(b):
                    return
                pe.wait_ge(xc_ready, NH * (b + 1))
                misc_free("xp", b)
                for h in range(NH):
                    last = T.matmul(misc_bank[0:XP, :], w_x[:, h], xc[:, h], start=(h == 0), stop=(h == NH - 1))
                last.then_inc(xp_ps, 1)

            def project_dt(b, h):
                if not live(b):
                    return
                pe.wait_ge(xp_ready, b + 1)
                misc_free(f"dt{h}", b)
                T.matmul(misc_bank[:], w_dt[:, P * h:P * h + P], xproj[0:DR, :], start=True,
                         stop=True).then_inc(dt_ps, 1)

            def start_y(b):
                if not live(b):
                    return
                pe.wait_ge(xcD_ready, b + 1)
                if begun(b):
                    pe.wait_ge(yg_ready, b)
                for h in range(NH):
                    for q in range(NQ):
                        last = T.matmul(y_ps[:, q, P * h:P * h + P], xcD[:, h, P * q:P * q + P], ident[:],
                                        start=(h == 0 and q % 2 == 0), stop=False, is_transpose=True,
                                        skip_group_check=True)
                last.then_inc(y_started, 1)

            def sum_unit(b, k):
                if not live(b):
                    return
                if isinstance(b, int) and b == 0:
                    busy(FILL)
                pe.wait_ge(hc_ready, UNITS * b + k + 1)
                h = k % NH
                for s in range(GS):
                    for q in range(NQ):
                        last = T.matmul(y_ps[:, q, P * h:P * h + P], hb[:, k % RING, s, P * q:P * q + P], ident[:],
                                        start=False, stop=(k >= UNITS - NH and s == GS - 1), is_transpose=True,
                                        skip_group_check=True)
                last.then_inc(sum_done, 1)

            def project_z(b, m):
                if not live(b):
                    return
                pe.wait_ge(xnT_ready, b + 1)
                misc_free(f"z{m}", b)
                for q in range(2):
                    t = TAPS - 1 + P * (2 * m + q)
                    last = T.matmul(misc_bank[:, DI * q:DI * q + DI], xnT[:, t:t + P], w_z[:], start=True, stop=True)
                last.then_inc(z_ps, 1)

            def transpose_y(b, h):
                if not live(b):
                    return
                pe.wait_ge(yg_ready, b + 1)
                misc_free(f"yT{h}", b)
                transposed(lambda q: yg[:, q, P * h:P * h + P], misc_bank, yT_ps)

            def project_out(b):
                if not live(b):
                    return
                pe.wait_ge(yT_ready, NH * (b + 1))
                misc_free("o", b)
                for q in range(NQ):
                    for h in range(NH):
                        last = T.matmul(misc_bank[:, DM * q:DM * q + DM], ygT[:, h, P * q:P * q + P], w_out[:, h],
                                        start=(h == 0), stop=(h == NH - 1))
                last.then_inc(o_ps, 1)

            def transpose_x1(b):
                if not live(b):
                    return
                pe.wait_ge(x1n_ready, b + 1)
                misc_free("x1T", b)
                transposed(lambda q: x1n[:, q], misc_bank, x1T_ps)

            def logits(b):
                if not live(b):
                    return
                pe.wait_ge(x1T_ready, b + 1)
                misc_free("lg", b)
                for q in range(NQ):
                    last = T.matmul(misc_bank[:, NE * q:NE * q + NE], x1T[:, P * q:P * q + P], gate[:],
                                    start=True, stop=True)
                last.then_inc(lg_ps, 1)

            def transpose_w(b):
                if not live(b):
                    return
                pe.wait_ge(w_ready, b + 1)
                misc_free("wf", b)
                for q in range(NQ):
                    last = T.matmul(misc_bank[:, P * q:P * q + P], w_tok[:, q], ident[:],
                                    start=True, stop=True, is_transpose=True)
                last.then_inc(wf_ps, 1)

            def product(dst, hi, lo, done):
                T.matmul(dst, hi, x1T_lo[:], start=True, stop=False)
                T.matmul(dst, lo, x1T_hi[:], start=False, stop=False)
                T.matmul(dst, hi, x1T_hi[:], start=False, stop=True).then_inc(done, 1)

            def gate_tile(b, j):
                if not live(b):
                    return
                rows = SHARED[j] if j < NSH else P
                hi, lo = ((w[:, P * j:P * j + rows] for w in (s_gate_hi, s_gate_lo)) if j < NSH else
                          (w[:, :, j - NSH] for w in (w_gate_hi, w_gate_lo)))
                if j == 0:
                    pe.wait_ge(x1T_split, b + 1)
                    if isinstance(b, int) and b == 0:
                        pe.wait_ge(w_split, 4)
                if begun(TILES * b + j - 1):
                    pe.wait_ge(silu_ready, TILES * b + j - 1)
                product(g_ps[0:rows, j % 2], hi, lo, gate_ps)

            def up_tile(b, j):
                if not live(b):
                    return
                rows = SHARED[j] if j < NSH else P
                hi, lo = ((w[:, P * j:P * j + rows] for w in (s_up_hi, s_up_lo)) if j < NSH else
                          (w[:, :, j - NSH] for w in (w_up_hi, w_up_lo)))
                if j == 0:
                    pe.wait_ge(x1T_split, b + 1)
                    if isinstance(b, int) and b == 0:
                        pe.wait_ge(w_split, 4)
                if begun(TILES * b + j - 1):
                    pe.wait_ge(act_ready, TILES * b + j - 1)
                product(u_ps[0:rows, j % 2], hi, lo, up_ps)

            def down(b, j):
                if not live(b):
                    return
                if j == 0:
                    if begun(b):
                        pe.wait_ge(f_taken, b)
                if j < NSH:
                    rows, w = SHARED[j], s_down[0:SHARED[j], j]
                    pe.wait_ge(act_ready, TILES * b + j + 1)
                else:
                    rows, w = P, w_down[:, j - NSH]
                    pe.wait_ge(actw_ready, ROUTED * b + j - NSH + 1)
                for q in range(NQ):
                    last = T.matmul(f_ps[:, q], act[0:rows, j % AR, P * q:P * q + P], w,
                                    start=(j == 0 and q == 0), stop=(j == TILES - 1), skip_group_check=True)
                last.then_inc(down_done, 1)

            pe.wait_ge(const_ready, 2)
            busy(WARM)
            transpose_xn(0, first=True)
            pe.wait_ge(early_loaded, 16 * EARLY)
            pe.wait_ge(w_taps_ready, 1)
            pe.wait_ge(zeros_ready, 1)

            def iteration(i):
                nxt, cur, old, older = i + 1, i, i - 1, i - 2
                sum_unit(old, 5)
                gate_tile(older, 2)
                transpose_w(older)
                gate_tile(older, 3)
                up_tile(older, 2)
                gate_tile(older, 4)
                sum_unit(old, 6)
                up_tile(older, 3)
                up_tile(older, 4)
                down(older, 0)
                sum_unit(old, 7)
                gate_tile(older, 5)
                down(older, 1)
                transpose_y(old, 0)
                up_tile(older, 5)
                down(older, 2)
                transpose_y(old, 1)
                gate_tile(older, 6)
                up_tile(older, 6)
                project_z(cur, 0)
                gate_tile(older, 7)
                project_z(cur, 1)
                up_tile(older, 7)
                gate_tile(older, 8)
                project_out(old)
                start_y(cur)
                up_tile(older, 8)
                transpose_xn(nxt)
                down(older, 3)
                sum_unit(cur, 0)
                gate_tile(older, 9)
                up_tile(older, 9)
                gate_tile(older, 10)
                project_xi(nxt, 0)
                sum_unit(cur, 1)
                down(older, 4)
                gate_tile(older, 11)
                project_xi(nxt, 1)
                up_tile(older, 10)
                sum_unit(cur, 2)
                down(older, 5)
                up_tile(older, 11)
                down(older, 6)
                project_x(nxt)
                gate_tile(older, 12)
                down(older, 7)
                up_tile(older, 12)
                gate_tile(older, 13)
                up_tile(older, 13)
                transpose_x1(old)
                sum_unit(cur, 3)
                down(older, 8)
                logits(old)
                down(older, 9)
                down(older, 10)
                project_dt(nxt, 0)
                down(older, 11)
                down(older, 12)
                project_dt(nxt, 1)
                up_tile(old, 0)
                gate_tile(old, 0)
                down(older, 13)
                sum_unit(cur, 4)
                gate_tile(old, 1)
                up_tile(old, 1)

            run(pe, iteration)


_INS = ["L0_attn_x", "L0_attn_W_in", "L0_attn_conv_w", "L0_attn_conv_b", "L0_attn_W_x", "L0_attn_W_dt",
        "L0_attn_b_dt", "L0_attn_A_log", "L0_attn_D", "L0_attn_W_out", "L0_ffn_gate_w", "L0_ffn_wg",
        "L0_ffn_wu", "L0_ffn_wd", "L0_ffn_swg", "L0_ffn_swu", "L0_ffn_swd"]
_OUTS = [((8, 512, 128), "float32")]


def kernel(**inputs):
    import numpy as _np
    import concourse.bacc as _bacc
    from concourse import mybir as _mybir
    from concourse.bass_utils import run_bass_kernel_spmd as _run

    nc = _bacc.Bacc("TRN2", target_bir_lowering=False, num_devices=1)
    arrays, args = {}, []
    for name in _INS:
        a = _np.ascontiguousarray(inputs[name])
        arrays[f"in_{name}_dram"] = a
        args.append(nc.dram_tensor(f"in_{name}_dram", a.shape, _mybir.dt.from_np(a.dtype), kind="ExternalInput").ap())
    for i, (shape, dtype) in enumerate(_OUTS):
        dt = _mybir.dt.from_np(_np.dtype(dtype))
        args.append(nc.dram_tensor(f"out_{i}_dram", shape, dt, kind="ExternalOutput").ap())
    layer_kernel(nc, *args)
    r = _run(nc, [arrays], core_ids=[0])
    got = tuple(r.results[0][f"out_{i}_dram"] for i in range(len(_OUTS)))
    return got[0]
```
